# Optimizing a Trainium2 kernel written in Bass

```python
import numpy as np
import jax
import jax.numpy as jnp

def _softmax(x, axis=-1):
    return jax.nn.softmax(x, axis=axis)

def _gelu(x):
    return jax.nn.gelu(x, approximate=True)

def _silu(x):
    return jax.nn.silu(x)

def _sigmoid(x):
    return jax.nn.sigmoid(x)

def _layernorm(x, axis=-1, eps=1e-05):
    m = jnp.mean(x, axis=axis, keepdims=True)
    v = jnp.var(x, axis=axis, keepdims=True)
    return (x - m) / jnp.sqrt(v + eps)

def _scatter_add(tgt, idx, src, axis=0):
    return tgt.at[idx].add(src)

def _segment_sum(src, seg, n):
    return jax.ops.segment_sum(src, seg, n)
kernel_name = 'mk_seq_preln_d1_jaxref_r8_6a4c3a'

def setup_inputs(seed: int=0):
    np.random.seed(seed)
    _w = jnp.asarray

    def _L0_attn_setup():
        import jax, jax.numpy as jnp
        import numpy as np
        ROPE_BASE = 10000.0

        def _rope_cos_sin(T, dh, dtype):
            inv_freq = 1.0 / ROPE_BASE ** (jnp.arange(0, dh, 2, dtype=jnp.float32) / dh)
            t = jnp.arange(T, dtype=jnp.float32)
            freqs = jnp.outer(t, inv_freq)
            emb = jnp.concatenate([freqs, freqs], axis=-1)
            return (jnp.cos(emb).astype(dtype), jnp.sin(emb).astype(dtype))

        def _rotate_half(x):
            x1, x2 = jnp.split(x, 2, axis=-1)
            return jnp.concatenate([-x2, x1], axis=-1)
        key = jax.random.key(seed)
        k1, k2, k3 = jax.random.split(key, 3)
        B, T, D = (2, 256, 256)
        x = jax.random.normal(k1, (B, T, D), dtype=jnp.float32)
        w_qkv = jax.random.normal(k2, (3 * D, D), dtype=jnp.float32) * D ** (-0.5)
        w_proj = jax.random.normal(k3, (D, D), dtype=jnp.float32) * D ** (-0.5)
        return {'x': x, 'w_qkv': w_qkv, 'w_proj': w_proj}
    _L0_attn_in = _L0_attn_setup()

    def _L0_ffn_setup():
        import jax, jax.numpy as jnp
        import numpy as np
        TOP_K = 8
        CAPACITY = 128
        key = jax.random.key(seed)
        k1, k2, k3, k4 = jax.random.split(key, 4)
        B, S, H, E, I = (2, 128, 256, 64, 96)
        hidden_states = jax.random.normal(k1, (B, S, H), dtype=jnp.float32)
        router_weight = jax.random.normal(k2, (E, H), dtype=jnp.float32) * 0.02
        gate_up_proj = jax.random.normal(k3, (E, H, 2 * I), dtype=jnp.float32) * 0.02
        down_proj = jax.random.normal(k4, (E, I, H), dtype=jnp.float32) * 0.02
        return {'hidden_states': hidden_states, 'router_weight': router_weight, 'gate_up_proj': gate_up_proj, 'down_proj': down_proj}
    _L0_ffn_in = _L0_ffn_setup()
    _d = {'L0_attn_x': _L0_attn_in['x'], 'L0_attn_w_qkv': _L0_attn_in['w_qkv'], 'L0_attn_w_proj': _L0_attn_in['w_proj'], 'L0_ffn_router_weight': _L0_ffn_in['router_weight'], 'L0_ffn_gate_up_proj': _L0_ffn_in['gate_up_proj'], 'L0_ffn_down_proj': _L0_ffn_in['down_proj']}
    _x0 = _d['L0_attn_x']
    _d['L0_attn_x'] = jax.random.normal(jax.random.fold_in(jax.random.key(seed), 1), (4, 512, 256), dtype=_x0.dtype)
    del _x0
    return _d

def reference(L0_attn_x, L0_attn_w_qkv, L0_attn_w_proj, L0_ffn_router_weight, L0_ffn_gate_up_proj, L0_ffn_down_proj):

    def _L0_attn_ref(x, w_qkv, w_proj):
        import jax, jax.numpy as jnp
        import numpy as np
        ROPE_BASE = 10000.0

        def _rope_cos_sin(T, dh, dtype):
            inv_freq = 1.0 / ROPE_BASE ** (jnp.arange(0, dh, 2, dtype=jnp.float32) / dh)
            t = jnp.arange(T, dtype=jnp.float32)
            freqs = jnp.outer(t, inv_freq)
            emb = jnp.concatenate([freqs, freqs], axis=-1)
            return (jnp.cos(emb).astype(dtype), jnp.sin(emb).astype(dtype))

        def _rotate_half(x):
            x1, x2 = jnp.split(x, 2, axis=-1)
            return jnp.concatenate([-x2, x1], axis=-1)
        B, T, D = x.shape
        H = 16
        Dh = D // H
        scale = Dh ** (-0.5)
        qkv = x @ w_qkv.T
        qkv = qkv.reshape(B, T, 3, H, Dh).transpose(2, 0, 3, 1, 4)
        q, k, v = (qkv[0], qkv[1], qkv[2])
        cos, sin = _rope_cos_sin(T, Dh, x.dtype)
        q = q * cos + _rotate_half(q) * sin
        k = k * cos + _rotate_half(k) * sin
        attn = jnp.einsum('bhqd,bhkd->bhqk', q, k) * scale
        causal = jnp.triu(jnp.full((T, T), -jnp.inf, dtype=attn.dtype), k=1)
        attn = jax.nn.softmax(attn + causal, axis=-1)
        out = jnp.einsum('bhqk,bhkd->bhqd', attn, v)
        out = out.transpose(0, 2, 1, 3).reshape(B, T, D)
        return out @ w_proj.T

    def _L0_ffn_ref(hidden_states, router_weight, gate_up_proj, down_proj):
        import jax, jax.numpy as jnp
        import numpy as np
        TOP_K = 8
        CAPACITY = 128
        B, S, H = hidden_states.shape
        E = router_weight.shape[0]
        K, C = (TOP_K, CAPACITY)
        x = hidden_states.reshape(-1, H)
        logits = x @ router_weight.T
        probs = jax.nn.softmax(logits, axis=-1)
        topw, topi = jax.lax.top_k(probs, K)
        topw = topw / jnp.sum(topw, axis=-1, keepdims=True)
        flat_e = topi.reshape(-1)
        oh = jax.nn.one_hot(flat_e, E, dtype=jnp.int32)
        pos = jnp.take_along_axis(jnp.cumsum(oh, axis=0), flat_e[:, None], axis=1)[:, 0] - 1
        x_rep = jnp.repeat(x, K, axis=0)
        xe = jnp.zeros((E, C, H), x.dtype).at[flat_e, pos].set(x_rep, mode='drop')
        gu = jnp.einsum('ech,ehf->ecf', xe, gate_up_proj)
        g, u = jnp.split(gu, 2, axis=-1)
        h = jax.nn.silu(g) * u
        ye = jnp.einsum('eci,eih->ech', h, down_proj)
        valid = pos < C
        y_flat = jnp.where(valid[:, None], ye[flat_e, jnp.minimum(pos, C - 1)], 0.0)
        y = jnp.sum(y_flat.reshape(-1, K, H) * topw.reshape(-1, K)[..., None], axis=1)
        return y.reshape(B, S, H)
    x = L0_attn_x
    x = x + _L0_attn_ref(_layernorm(x, axis=-1), L0_attn_w_qkv, L0_attn_w_proj)
    x = x + _L0_ffn_ref(_layernorm(x, axis=-1), L0_ffn_router_weight, L0_ffn_gate_up_proj, L0_ffn_down_proj)
    return x

_drawn_inputs = setup_inputs


def setup_inputs(seed=0):
    import zlib

    import numpy as np

    out = dict(_drawn_inputs(seed))
    spreads = {}
    factors = {'L0_ffn_router_weight': 8.0, 'L0_ffn_gate_up_proj': 8.0, 'L0_ffn_down_proj': 8.0}
    for name, (base, spread) in spreads.items():
        noise = np.random.default_rng([zlib.crc32(name.encode()), seed]).standard_normal(out[name].shape)
        drawn = base * np.exp(spread * noise) if base else spread * noise
        out[name] = jnp.asarray(drawn.astype(out[name].dtype))
    for name, factor in factors.items():
        out[name] = (out[name] * factor).astype(out[name].dtype)
    return out
```

```python
from contextlib import ExitStack

import numpy as np

import concourse.bass as bass
from concourse import mybir

F32 = mybir.dt.float32
BF16 = mybir.dt.bfloat16
F16 = mybir.dt.float16
I32 = mybir.dt.int32
U32 = mybir.dt.uint32
ALU = mybir.AluOpType
ACT = mybir.ActivationFunctionType
AX_X = mybir.AxisListType.X

P = 128
NB, T, D = 4, 512, 256
H, DH = 16, 16
E, I, K, CAP = 64, 96, 8, 128
TI = T // P
NT = NB * TI
NTOK = NB * T
HP = H // 2
DC = D // P
SCALE = DH ** -0.5
EPS = 1e-5
MASKED = -1e30
PAIRS_Q = (0, 0, 1, 1, 0, 2)
PAIRS_K = (0, 1, 0, 1, 2, 0)
SR = len(PAIRS_Q) * DH
VW = 3 * DH + 1
POFF = (0, 512, 896, 1152)
PW = 1280
GROUPS = ((0,), (1,), (2, 3))
XW = D + E
NACC = 2
ROWS = NTOK + P
U = 8
NR = E // U
NSET = 3 * (NACC - 1) + 1
ESH = 12

C_ID, C_MQ, C_MK, C_TRI, C_IO, C_EO, C_IE, C_TOK, C_DUM, C_ONE = 0, 128, 256, 384, 512, 640, 704, 768, 784, 785
NCONST = C_ONE + P


def constants():
    c = np.zeros((P, NCONST), np.float32)
    r, q = np.arange(P)[:, None], np.arange(P)[None, :]
    c[:, C_ID:C_ID + P] = r == q
    c[:, C_MQ:C_MQ + P] = np.where(q > r, MASKED, 0)
    c[:, C_MK:C_MK + P] = np.where(r > q, MASKED, 0)
    c[:, C_TRI:C_TRI + P] = r <= q
    c[:, C_IO:C_IO + P] = q + 1
    c[:, C_EO:C_EO + E] = np.arange(E) * 2.0 ** ESH
    c[:, C_IE:C_IE + E] = np.arange(E)
    c[:, C_TOK:C_TOK + NT] = r + 1 + P * np.arange(NT)
    c[:, C_DUM:C_DUM + 1] = NTOK + 1 + r
    c[:, C_ONE:] = 1.0
    inv = (1.0 / np.float32(10000.0) ** (np.arange(0, DH, 2, dtype=np.float32) / np.float32(DH))).astype(np.float32)
    f = np.outer(np.arange(T, dtype=np.float32), inv).astype(np.float32)
    emb = np.concatenate([f, f], -1)
    cos, sin = np.cos(emb).T, np.sin(emb).T
    sin = np.concatenate([-sin[:DH // 2], sin[DH // 2:]], 0)
    rot = np.stack([np.tile(cos, (P // DH, 1)), np.tile(sin, (P // DH, 1))], 1).astype(np.float32)
    return c, rot


def schedule():
    steps = [("prep", 0), ("rowmax", 0), ("prep", 1)]
    for b in range(NB):
        steps += [("attend", b), ("post", b)]
        if b + 2 < NB:
            steps.append(("prep", b + 2))
    return steps


def ring_uses():
    wide, narrow, out = [], [], []
    for step, b in schedule():
        if step == "prep":
            wide += [("xnT", b)] + [("rope", b, j) for j in range(4)]
            narrow += [("v", b, j) for j in range(2)]
        if step == "rowmax":
            wide += [("max", b, hp, i) for hp in range(HP) for i in range(TI)]
            narrow.append(("mT", b))
        if step == "attend":
            for h in range(H):
                if b + 1 < NB:
                    wide += [("max", b + 1, h // 2, 2 * (h % 2) + i) for i in range(2)]
                narrow += [("s", b, h, g) for g in range(len(GROUPS))]
                if h % 2 == 0 and h:
                    out.append(("out", b, h // 2 - 1))
            out.append(("out", b, HP - 1))
            if b + 1 < NB:
                narrow.append(("mT", b + 1))
        if step == "post":
            wide += [("attT", b), ("x2T", b)]
            narrow += [("proj", b, 0), ("proj", b, 1), ("router", b), ("count", b), ("table", b)]
    return [{key: n for n, key in enumerate(uses)} for uses in (wide, narrow, out)]


class Ring:

    def __init__(self, uses, slots, full, empty):
        self.uses, self.slots, self.full, self.empty = uses, slots, full, empty

    def slot(self, key):
        return self.slots[self.uses[key] % 2]

    def acquire(self, pe, key):
        n = self.uses[key]
        if n >= 2:
            pe.wait_ge(self.empty[n % 2], n // 2)
        return self.slot(key)

    def filled(self, ins, key):
        ins.then_inc(self.full[self.uses[key] % 2], 1)

    def wait_full(self, eng, key):
        n = self.uses[key]
        eng.wait_ge(self.full[n % 2], n // 2 + 1)
        return self.slot(key)

    def taken(self, ins, key):
        ins.then_inc(self.empty[self.uses[key] % 2], 1)

    def wait_taken(self, eng, key):
        n = self.uses[key]
        eng.wait_ge(self.empty[n % 2], n // 2 + 1)


def on_pool(h):
    return h % 2 == 1


def build(nc, x, wqk, wv, wp, wr, gup, dnp, cst, rot, out):
    qk_d = [nc.dram_tensor(f"qk_parts{s}", (3, 2 * D, T), BF16, kind="Internal").ap() for s in range(2)]
    m_d = [nc.dram_tensor(f"neg_max{s}", (2 * H, T), BF16, kind="Internal").ap() for s in range(2)]
    xw_d = nc.dram_tensor("token_rows", (NTOK, XW), F32, kind="Internal").ap()
    acc_d = [nc.dram_tensor(f"acc{s}", (ROWS, D), F32, kind="Internal").ap() for s in range(NACC)]

    top = ExitStack()
    with top:
        def keep_sb(name, shape, dt):
            return top.enter_context(nc.sbuf_tensor(name, shape, dt))

        def sem(name):
            return top.enter_context(nc.semaphore(name))

        banks = top.enter_context(nc.psum_tensor("banks", [P, 8, 512], F32))
        consts = keep_sb("consts", [P, NCONST], F32)
        idf = consts[:, C_ID:C_ID + P]
        table = keep_sb("table", [P, E], F32)
        rows_of = keep_sb("rows_of", [P, E, 2], U32)
        const_in = sem("const_in")
        rows_stored = sem("rows_stored")
        acc_set = sem("acc_set")
        rows_done = sem("rows_done")

        gup_v = gup.rearrange("e (p c) f -> p e c f", c=DC)
        dnp_v = dnp.rearrange("e i d -> i e d")

        attention(nc, x, wqk, wv, wp, wr, cst, rot, qk_d, m_d, xw_d, acc_d, banks, consts, table, rows_of,
                  const_in, rows_stored, acc_set, rows_done)
        experts(nc, xw_d, acc_d, banks, idf, rows_of, gup_v, dnp_v, out)


def attention(nc, x, wqk, wv, wp, wr, cst, rot, qk_d, m_d, xw_d, acc_d, banks, consts, table, rows_of,
              const_in, rows_stored, acc_set, rows_done):
    ctx = ExitStack()
    with ctx:
        def sb(name, shape, dt):
            return ctx.enter_context(nc.sbuf_tensor(name, shape, dt))

        def sem(name):
            return ctx.enter_context(nc.semaphore(name))

        idf = consts[:, C_ID:C_ID + P]
        cb = sb("consts_bf16", [P, NCONST], BF16)
        rot_sb = sb("rot_sb", [P, 2, T], F32)
        wqk_sb = sb("wqk_sb", [P, DC, 4 * D], F32)
        wv_sb = sb("wv_sb", [P, DC, D], F32)
        wp_sb = sb("wp_sb", [P, DC, D], F32)
        wr_sb = sb("wr_sb", [P, DC, E], F32)
        xs = sb("xs", [P, NT, D], F32)
        xn = sb("xn", [P, TI, D], F32)
        xT = sb("xT", [P, DC, T], F32)
        stats = sb("stats", [P, TI, 6], F32)
        mv = sb("mv", [P, TI, 2], F32)
        vpe = sb("vpe", [P, TI], F32)
        half = sb("half", [P, TI], F32)
        rstd = sb("rstd", [P, TI], F32)
        work = sb("work", [P, 8 * T], F32)
        rc = work[:, 0:4 * T].rearrange("p (s r t) -> p s r t", s=2, r=2)
        qk = work[:, 4 * T:6 * T].rearrange("p (s t) -> p s t", s=2)
        resid = work[:, 6 * T:8 * T].rearrange("p (s t) -> p s t", s=2)
        ohc = work[:, 0:4 * T].bitcast(F16).rearrange("p (n c) -> p n c", c=CAP)
        ohe = work[:, 4 * T:6 * T].bitcast(F16).rearrange("p (n e) -> p n e", e=E)
        oht = work[:, 6 * T:8 * T].bitcast(F16).rearrange("p (n e) -> p n e", e=E)
        parts = sb("parts", [P, 3, 4, T], BF16)
        stq = [sb(f"stq{s}", [SR + 2, H, T], BF16) for s in range(2)]
        stk = [sb(f"stk{s}", [SR + 2, H, T], BF16) for s in range(2)]
        vst = [sb(f"vst{s}", [P, TI, H, VW], BF16) for s in range(2)]
        vres = sb("vres", [P, 2, D], F32)
        mx = sb("mx", [P, TI, H], F32)
        nm = sb("nm", [P, TI, 2, H], BF16)
        mT = sb("mT", [2 * H, T], BF16)
        prob = sb("prob", [P, 3, PW], F32)
        prob2 = sb("prob2", [P, 3, PW], BF16)
        red = sb("red", [P, 2 * TI, DH], F32)
        rden = sb("rden", [P, 2 * TI], F32)
        att = sb("att", [P, TI, D], F32)
        attT = sb("attT", [P, DC, T], F32)
        xw = sb("xw", [P, TI, XW], F32)
        lv = sb("lv", [P, TI, E + K], F32)
        lrep = sb("lrep", [P, TI, E], F32)
        ev = sb("ev", [P, TI, E + K], F32)
        wsum = sb("wsum", [P, TI], F32)
        chosen = sb("chosen", [P, TI, E], BF16)
        before = sb("before", [P, TI + 1, E], BF16)
        comp = sb("comp", [P, TI, E], F32)
        comp8 = sb("comp8", [P, TI, K], F32)
        compi = sb("compi", [P, TI * K], I32)
        eki = sb("eki", [P, 2, TI * K], I32)
        ekf = sb("ekf", [P, 2, TI * K], F32)

        wide_uses, narrow_uses, out_uses = ring_uses()

        def ring(name, uses, slots):
            return Ring(uses, slots, [sem(f"{name}_full{s}") for s in range(2)],
                        [sem(f"{name}_empty{s}") for s in range(2)])

        wide = ring("wide", wide_uses, [banks[:, 0:2, :], banks[:, 2:4, :]])
        narrow = ring("narrow", narrow_uses, [banks[:, 4, :], banks[:, 5, :]])
        outr = ring("out", out_uses, [banks[:, 6, :], banks[:, 7, :]])

        x_in, w_in = sem("x_in"), sem("w_in")
        cast_done, ones_set, half_set = sem("cast_done"), sem("ones_set"), sem("half_set")
        stats_done, var_done, eps_done, rstd_done, norm_done = (
            sem("stats_done"), sem("var_done"), sem("eps_done"), sem("rstd_done"), sem("norm_done"))
        summed, part1, residual, part2, part3 = (
            sem("summed"), sem("part1"), sem("residual"), sem("part2"), sem("part3"))
        v1_done, v2_done, v3_done = sem("v1_done"), sem("v2_done"), sem("v3_done")
        stored = sem("stored")
        loaded = [sem(f"loaded{s}") for s in range(2)]
        nm_done, m_stored = sem("nm_done"), sem("m_stored")
        m_loaded = [sem(f"m_loaded{s}") for s in range(2)]
        p2_dve, p2_pool, pv_done = sem("p2_dve"), sem("p2_pool"), sem("pv_done")
        att_done = sem("att_done")
        norm2_done = sem("norm2_done")
        dve = sem("dve_step")
        xw_done, ev_done, lvs_done = sem("xw_done"), sem("ev_done"), sem("lvs_done")
        chosen_done, onehot_done = sem("chosen_done"), sem("onehot_done")
        zero_set = sem("zero_set")

        maskq, maskk = cb[:, C_MQ:C_MQ + P], cb[:, C_MK:C_MK + P]
        idb, tri, onesb = cb[:, C_ID:C_ID + P], cb[:, C_TRI:C_TRI + P], cb[:, C_ONE:C_ONE + P]

        NLOAD = 2 * len(PAIRS_Q)

        def second_part(eng, queue, b, h, done):
            n = b * H + h
            narrow.wait_taken(queue, ("s", b, h, len(GROUPS) - 1))
            if n >= 3:
                queue.wait_ge(pv_done, n - 2)
            eng.tensor_tensor(prob2[:, n % 3, :], prob[:, n % 3, :], prob_lead(n % 3), ALU.subtract).then_inc(done, 1)

        def prob_lead(s):
            return prob[:, s, :].bitcast(BF16).rearrange("p (n t) -> p n t", t=2)[:, :, 1]

        with nc.Block() as block:
            @block.sync
            def _(sp):
                xv = x.rearrange("(b i p) d -> b p i d", b=NB, p=P)
                sp.dma_start(xs[:, 0:TI, :], xv[0]).then_inc(x_in, 16)
                sp.dma_start(consts[:], cst).then_inc(const_in, 16)
                sp.dma_start(wqk_sb[:], wqk.rearrange("(c p) n -> p c n", c=DC)).then_inc(w_in, 16)
                sp.dma_start(rot_sb[:], rot).then_inc(w_in, 16)
                sp.dma_start(wv_sb[:], wv.rearrange("(c p) n -> p c n", c=DC)).then_inc(w_in, 16)
                sp.dma_start(wp_sb[:], wp.rearrange("(c p) n -> p c n", c=DC)).then_inc(w_in, 16)
                sp.dma_start(wr_sb[:], wr.rearrange("(c p) n -> p c n", c=DC)).then_inc(w_in, 16)
                sp.wait_ge(x_in, 16)
                for b in range(1, NB):
                    sp.dma_start(xs[:, b * TI:(b + 1) * TI, :], xv[b]).then_inc(x_in, 16)
                sp.wait_ge(zero_set, 1)
                zeros = prob[:].rearrange("p s n -> p (s n)")
                for a in range(1, NACC):
                    sp.dma_start(acc_d[a][0:NTOK // 2, :].rearrange("(p r) d -> p (r d)", p=P),
                                 zeros[:, 0:NT // 2 * D]).then_inc(acc_set, 16)
                    sp.dma_start(acc_d[a][NTOK // 2:NTOK, :].rearrange("(p r) d -> p (r d)", p=P),
                                 zeros[:, 0:NT // 2 * D]).then_inc(acc_set, 16)
                    sp.dma_start(acc_d[a][NTOK:ROWS, :], zeros[:, 0:D]).then_inc(acc_set, 16)
                sp.dma_start(acc_d[0][NTOK:ROWS, :], zeros[:, 0:D]).then_inc(acc_set, 16)
                for step, b in schedule():
                    s = b % 2
                    if step == "prep":
                        if b >= 2:
                            sp.wait_ge(pv_done, H * (b - 1))
                        sp.wait_ge(part3, 4 * (b + 1))
                        for r in range(3):
                            sp.dma_start(qk_d[s][r].rearrange("(j p) t -> p j t", p=P),
                                         parts[:, r, :, :]).then_inc(stored, 16)
                        sp.wait_ge(stored, 48 * (b + 1))
                        for g in range(len(PAIRS_Q)):
                            for st, pr, o in ((stq, PAIRS_Q, 0), (stk, PAIRS_K, D)):
                                src = qk_d[s][pr[g], o:o + D, :].rearrange("(h d) t -> d h t", d=DH)
                                sp.dma_start(st[s][g * DH:(g + 1) * DH, :, :], src).then_inc(loaded[s], 16)
                    nb = b if step == "rowmax" else b + 1
                    if step == "rowmax" or (step == "attend" and b + 1 < NB):
                        narrow.wait_taken(sp, ("mT", nb))
                        sp.dma_start(m_d[nb % 2], mT[:]).then_inc(m_stored, 16)
                        sp.wait_ge(m_stored, 16 * (nb + 1))
                        sp.dma_start(stq[nb % 2][SR:SR + 2, :, :],
                                     m_d[nb % 2].rearrange("(r h) t -> r h t", r=2)).then_inc(m_loaded[nb % 2], 16)
                    if step == "post":
                        for j in range(2):
                            narrow.wait_taken(sp, ("proj", b, j))
                        sp.wait_ge(acc_set, 16 * (NSET + b))
                        sp.dma_start(acc_d[0][b * T:(b + 1) * T, :].rearrange("(i p) d -> p i d", p=P),
                                     xs[:, b * TI:(b + 1) * TI, :]).then_inc(acc_set, 16)
                        sp.wait_ge(xw_done, b + 1)
                        sp.dma_start(xw_d[b * T:(b + 1) * T, :].rearrange("(i p) d -> p i d", p=P),
                                     xw[:]).then_inc(rows_stored, 16)
                sp.wait_ge(rows_stored, 16 * NB)
                sp.wait_ge(acc_set, 16 * (NSET + NB))

            @block.gpsimd
            def _(pool):
                nc.gpsimd.memset(prob[:], 0.0).then_inc(zero_set, 1)
                nc.gpsimd.memset(half[:], -0.5).then_inc(half_set, 1)
                nc.gpsimd.memset(table[:], 0.0).then_inc(half_set, 1)
                nc.gpsimd.memset(before[:], 0.0).then_inc(half_set, 1)
                for s in range(2):
                    nc.gpsimd.memset(vst[s][:, :, :, 3 * DH:VW], 1.0).then_inc(ones_set, 1)
                pool.wait_ge(half_set, 3)
                norms = [0]

                def root():
                    norms[0] += 1
                    n = norms[0]
                    pool.wait_ge(var_done, n)
                    nc.gpsimd.tensor_scalar(vpe[:], mv[:, :, 1], EPS, None, ALU.add).then_inc(eps_done, 1)
                    pool.wait_ge(eps_done, n)
                    nc.gpsimd.tensor_tensor(rstd[:], vpe[:], half[:], ALU.pow).then_inc(rstd_done, 1)

                def add(b, j):
                    n = 4 * b + j
                    wide.wait_taken(pool, ("rope", b, j))
                    if n >= 2:
                        pool.wait_ge(residual, n - 1)
                    nc.gpsimd.tensor_tensor(qk[:, j % 2, :], rc[:, j % 2, 0, :], rc[:, j % 2, 1, :],
                                            ALU.add).then_inc(summed, 1)

                def first_residual(b, j):
                    n = 4 * b + j
                    pool.wait_ge(part1, n + 1)
                    if n >= 2:
                        pool.wait_ge(part3, n - 1)
                    nc.gpsimd.tensor_tensor(resid[:, j % 2, :], qk[:, j % 2, :], parts[:, 0, j, :],
                                            ALU.subtract).then_inc(residual, 1)

                def third_part(b, j):
                    pool.wait_ge(part2, 4 * b + j + 1)
                    nc.gpsimd.tensor_tensor(parts[:, 2, j, :], resid[:, j % 2, :], parts[:, 1, j, :],
                                            ALU.subtract).then_inc(part3, 1)

                for step, b in schedule():
                    if step == "prep":
                        root()
                        for j in range(6):
                            if j < 4:
                                add(b, j)
                            if 1 <= j < 5:
                                first_residual(b, j - 1)
                            if j >= 2:
                                third_part(b, j - 2)
                    if step == "attend":
                        for h in range(H):
                            if on_pool(h):
                                second_part(nc.gpsimd, pool, b, h, p2_pool)
                    if step == "post":
                        root()

            @block.scalar
            def _(act):
                for step, b in schedule():
                    s = b % 2
                    if step == "prep":
                        ps = wide.wait_full(act, ("xnT", b))
                        if b:
                            narrow.wait_full(act, ("v", b - 1, 1))
                        nc.scalar.copy(xT[:, 0, :], ps[:, 0, :])
                        wide.taken(nc.scalar.copy(xT[:, 1, :], ps[:, 1, :]), ("xnT", b))

                        def first_part(j):
                            act.wait_ge(summed, 4 * b + j + 1)
                            nc.scalar.copy(parts[:, 0, j, :], qk[:, j % 2, :]).then_inc(part1, 1)

                        def second_part_qk(j):
                            act.wait_ge(residual, 4 * b + j + 1)
                            nc.scalar.copy(parts[:, 1, j, :], resid[:, j % 2, :]).then_inc(part2, 1)

                        if b:
                            act.wait_ge(stored, 48 * b)
                        for j in range(5):
                            if j < 4:
                                first_part(j)
                            if j >= 1:
                                second_part_qk(j - 1)
                        for j in range(2):
                            ps = narrow.wait_full(act, ("v", b, j))
                            if b >= 2 and j == 0:
                                act.wait_ge(pv_done, H * (b - 1))
                            dst = vst[s][:, 2 * j:2 * j + 2, :, :]
                            for i in range(2):
                                ins = nc.scalar.copy(dst[:, i, :, 0:DH],
                                                     ps[:, i * D:(i + 1) * D].rearrange("p (h d) -> p h d", d=DH))
                            ins.then_inc(v1_done, 1)
                            narrow.wait_taken(act, ("v", b, j))
                            for i in range(2):
                                ins = nc.scalar.copy(dst[:, i, :, DH:2 * DH],
                                                     vres[:, i, :].rearrange("p (h d) -> p h d", d=DH))
                            ins.then_inc(v2_done, 1)
                    if step == "attend":
                        for h in range(H):
                            n = b * H + h
                            for g, tiles in enumerate(GROUPS):
                                ps = narrow.wait_full(act, ("s", b, h, g))
                                if g == 0 and n >= 3:
                                    act.wait_ge(pv_done, n - 2)
                                if g == 0 and n == 0:
                                    act.wait_ge(acc_set, 16 * NSET)
                                w = sum(T - P * j for j in tiles)
                                o = POFF[tiles[0]]
                                narrow.taken(nc.scalar.activation(prob[:, n % 3, o:o + w], ps[:, 0:w], ACT.Exp,
                                                                  scale=SCALE), ("s", b, h, g))
                    if step in ("rowmax", "attend"):
                        nb = b if step == "rowmax" else b + 1
                        if nb < NB:
                            ps = narrow.wait_full(act, ("mT", nb))
                            if nb:
                                act.wait_ge(m_stored, 16 * nb)
                            narrow.taken(nc.scalar.copy(mT[:], ps[0:2 * H, 0:T // 2].bitcast(BF16)), ("mT", nb))
                    if step == "post":
                        ps = wide.wait_full(act, ("attT", b))
                        nc.scalar.copy(attT[:, 0, :], ps[:, 0, :])
                        wide.taken(nc.scalar.copy(attT[:, 1, :], ps[:, 1, :]), ("attT", b))
                        ps = wide.wait_full(act, ("x2T", b))
                        nc.scalar.copy(attT[:, 0, :], ps[:, 0, :])
                        wide.taken(nc.scalar.copy(attT[:, 1, :], ps[:, 1, :]), ("x2T", b))
                        ps = narrow.wait_full(act, ("router", b))
                        narrow.taken(nc.scalar.copy(lv[:, :, 0:E], ps[:, 0:TI * E].rearrange("p (i e) -> p i e", e=E)),
                                     ("router", b))
                        act.wait_ge(lvs_done, b + 1)
                        nc.scalar.activation(ev[:], lv[:], ACT.Exp).then_inc(ev_done, 1)

            @block.tensor
            def _(pe):
                pe.wait_ge(cast_done, 1)

                def transposes(key, src):
                    ps = wide.acquire(pe, key)
                    for i in range(TI):
                        for c in range(DC):
                            ins = nc.tensor.transpose(ps[:, c, i * P:(i + 1) * P], src[:, i, c * P:(c + 1) * P], idf)
                    wide.filled(ins, key)

                def prep(b):
                    pe.wait_ge(norm_done, b + 1)
                    transposes(("xnT", b), xn)
                    wide.wait_taken(pe, ("xnT", b))
                    if b == 0:
                        pe.wait_ge(w_in, 16 * 5)
                    for j in range(4):
                        ps = wide.acquire(pe, ("rope", b, j))
                        for r in range(2):
                            o = r * 2 * D + j * P
                            for c in range(DC):
                                ins = nc.tensor.matmul(ps[:, r, :], wqk_sb[:, c, o:o + P], xT[:, c, :],
                                                       start=(c == 0), stop=(c == DC - 1))
                        wide.filled(ins, ("rope", b, j))
                    for j in range(2):
                        ps = narrow.acquire(pe, ("v", b, j))
                        for i in range(2):
                            for c in range(DC):
                                ins = nc.tensor.matmul(ps[:, i * D:(i + 1) * D],
                                                       xT[:, c, (2 * j + i) * P:(2 * j + i + 1) * P], wv_sb[:, c, :],
                                                       start=(c == 0), stop=(c == DC - 1))
                        narrow.filled(ins, ("v", b, j))

                def row_max(b, hp, i):
                    s, w = b % 2, (i + 1) * P
                    if hp == 0 and i == 0:
                        pe.wait_ge(loaded[s], 16 * NLOAD * (b // 2 + 1))
                    ps = wide.acquire(pe, ("max", b, hp, i))
                    for j in range(2):
                        h = 2 * hp + j
                        nc.tensor.matmul(ps[:, j, i * P:w], idb, maskq, start=True, stop=False,
                                         skip_group_check=True)
                        ins = nc.tensor.matmul(ps[:, j, 0:w], stq[s][0:SR, h, i * P:w], stk[s][0:SR, h, 0:w],
                                               start=False, stop=True, skip_group_check=True)
                    wide.filled(ins, ("max", b, hp, i))

                def max_rows(b):
                    pe.wait_ge(nm_done, b + 1)
                    ps = narrow.acquire(pe, ("mT", b))[0:2 * H, 0:T // 2].bitcast(BF16)
                    for i in range(TI):
                        ins = nc.tensor.transpose(ps[:, i * P:(i + 1) * P],
                                                  nm[:, i, :, :].rearrange("p r h -> p (r h)"), idb)
                    narrow.filled(ins, ("mT", b))

                def scores(b, h):
                    s = b % 2
                    for g, tiles in enumerate(GROUPS):
                        ps = narrow.acquire(pe, ("s", b, h, g))
                        o = 0
                        for j in tiles:
                            w = T - j * P
                            nc.tensor.matmul(ps[:, o:o + P], idb, maskk, start=True, stop=False,
                                             skip_group_check=True)
                            ins = nc.tensor.matmul(ps[:, o:o + w], stk[s][:, h, j * P:(j + 1) * P],
                                                   stq[s][:, h, j * P:T], start=False, stop=True,
                                                   skip_group_check=True)
                            o += w
                        narrow.filled(ins, ("s", b, h, g))

                def attend_head(b, h):
                    n, s = b * H + h, b % 2
                    if on_pool(h):
                        pe.wait_ge(p2_pool, n // 2 + 1)
                    else:
                        pe.wait_ge(p2_dve, n // 2 + 1)
                    key = ("out", b, h // 2)
                    ps = outr.acquire(pe, key) if h % 2 == 0 else outr.slot(key)
                    lead, rest = prob_lead(n % 3), prob2[:, n % 3, :]
                    for i in range(TI):
                        o = (h % 2 * TI + i) * VW
                        for j in range(i + 1):
                            c = POFF[j] + (i - j) * P
                            for part in (lead, rest):
                                ins = nc.tensor.matmul(ps[:, o:o + VW], part[:, c:c + P], vst[s][:, j, h, :],
                                                       start=(j == 0 and part is lead),
                                                       stop=(j == i and part is rest), skip_group_check=True)
                        if i == TI - 1:
                            ins.then_inc(pv_done, 1)

                def post(b):
                    pe.wait_ge(att_done, HP * (b + 1))
                    transposes(("attT", b), att)
                    wide.wait_taken(pe, ("attT", b))
                    for j in range(2):
                        ps = narrow.acquire(pe, ("proj", b, j))
                        for i in range(2):
                            for c in range(DC):
                                ins = nc.tensor.matmul(ps[:, i * D:(i + 1) * D],
                                                       attT[:, c, (2 * j + i) * P:(2 * j + i + 1) * P], wp_sb[:, c, :],
                                                       start=(c == 0), stop=(c == DC - 1))
                        narrow.filled(ins, ("proj", b, j))
                    pe.wait_ge(norm2_done, b + 1)
                    transposes(("x2T", b), xw)
                    wide.wait_taken(pe, ("x2T", b))
                    ps = narrow.acquire(pe, ("router", b))
                    for i in range(TI):
                        for c in range(DC):
                            ins = nc.tensor.matmul(ps[:, i * E:(i + 1) * E], attT[:, c, i * P:(i + 1) * P],
                                                   wr_sb[:, c, :], start=(c == 0), stop=(c == DC - 1))
                    narrow.filled(ins, ("router", b))
                    pe.wait_ge(chosen_done, b + 1)
                    ps = narrow.acquire(pe, ("count", b))
                    for i in range(TI):
                        nc.tensor.matmul(ps[:, i * E:(i + 1) * E], tri, chosen[:, i, :], start=True, stop=False)
                        ins = nc.tensor.matmul(ps[:, i * E:(i + 1) * E], onesb, before[:, i, :], start=False, stop=True)
                    narrow.filled(ins, ("count", b))
                    pe.wait_ge(onehot_done, b + 1)
                    ps = narrow.acquire(pe, ("table", b))
                    for n in range(TI * K):
                        ins = nc.tensor.matmul(ps[:, 0:E], ohc[:, n, :], oht[:, n, :], start=(n == 0),
                                               stop=(n == TI * K - 1))
                    narrow.filled(ins, ("table", b))

                for step, b in schedule():
                    if step == "prep":
                        prep(b)
                    if step == "rowmax":
                        for hp in range(HP):
                            for i in range(TI):
                                row_max(b, hp, i)
                        max_rows(b)
                    if step == "attend":
                        pe.wait_ge(m_loaded[b % 2], 16 * (b // 2 + 1))
                        if b == 0:
                            pe.wait_ge(ones_set, 2)
                        pe.wait_ge(v3_done, 2 * (b + 1))
                        for h in range(H):
                            scores(b, h)
                            if b + 1 < NB:
                                for i in range(2):
                                    row_max(b + 1, h // 2, 2 * (h % 2) + i)
                            if h:
                                attend_head(b, h - 1)
                        attend_head(b, H - 1)
                        if b + 1 < NB:
                            max_rows(b + 1)
                    if step == "post":
                        post(b)

            @block.vector
            def _(vec):
                v = nc.vector
                step_n = [0]

                def link(ins):
                    step_n[0] += 1
                    ins.then_inc(dve, 1)
                    vec.wait_ge(dve, step_n[0])

                for s in range(2):
                    v.memset(stk[s][SR:SR + 2, :, :], 1.0)
                vec.wait_ge(const_in, 16)
                v.tensor_copy(cb[:], consts[:]).then_inc(cast_done, 1)
                norms = [0]

                def normalise(src, dst, done):
                    norms[0] += 1
                    n = norms[0]
                    for i in range(TI):
                        ins = v.bn_stats(stats[:, i, :], src[:, i, :])
                    link(ins)
                    for i in range(TI):
                        ins = v.bn_aggr(mv[:, i, :], stats[:, i, :])
                    ins.then_inc(var_done, 1)
                    vec.wait_ge(rstd_done, n)
                    for i in range(TI):
                        ins = v.tensor_scalar(dst[:, i, 0:D], src[:, i, :], mv[:, i, 0:1], rstd[:, i:i + 1],
                                              ALU.subtract, ALU.mult)
                    ins.then_inc(done, 1)

                def prep(b):
                    vec.wait_ge(x_in, 16 if b == 0 else 16 * NB)
                    if b:
                        wide.wait_full(vec, ("xnT", b - 1))
                    normalise(xs[:, b * TI:(b + 1) * TI, :], xn, norm_done)
                    if b == 0:
                        vec.wait_ge(w_in, 16 * 5)
                    for j in range(4):
                        ps = wide.wait_full(vec, ("rope", b, j))
                        n = 4 * b + j
                        if n >= 2:
                            vec.wait_ge(summed, n - 1)
                        v.tensor_tensor(rc[:, j % 2, 0, :], ps[:, 0, :], rot_sb[:, 0, :], ALU.mult)
                        wide.taken(v.tensor_tensor(rc[:, j % 2, 1, :], ps[:, 1, :], rot_sb[:, 1, :], ALU.mult),
                                   ("rope", b, j))
                    for j in range(2):
                        n = 2 * b + j
                        dst = vst[b % 2][:, 2 * j:2 * j + 2, :, :]
                        vec.wait_ge(v1_done, n + 1)
                        if n:
                            vec.wait_ge(v2_done, n)
                            vec.wait_ge(v3_done, n)
                        ps = narrow.wait_full(vec, ("v", b, j))
                        for i in range(2):
                            ins = v.tensor_tensor(vres[:, i, :].rearrange("p (h d) -> p h d", d=DH),
                                                  ps[:, i * D:(i + 1) * D].rearrange("p (h d) -> p h d", d=DH),
                                                  dst[:, i, :, 0:DH], ALU.subtract)
                        narrow.taken(ins, ("v", b, j))
                        vec.wait_ge(v2_done, n + 1)
                        for i in range(2):
                            ins = v.tensor_tensor(dst[:, i, :, 2 * DH:3 * DH],
                                                  vres[:, i, :].rearrange("p (h d) -> p h d", d=DH),
                                                  dst[:, i, :, DH:2 * DH], ALU.subtract)
                        ins.then_inc(v3_done, 1)

                def row_max(b, hp, i):
                    ps = wide.wait_full(vec, ("max", b, hp, i))
                    if b and hp == 0 and i == 0:
                        vec.wait_ge(nm_done, b)
                    wide.taken(v.tensor_reduce(mx[:, i, 2 * hp:2 * hp + 2], ps[:, :, 0:(i + 1) * P], AX_X, ALU.max),
                               ("max", b, hp, i))

                def negate_max(b):
                    for i in (2, 3):
                        wide.wait_taken(vec, ("max", b, HP - 1, i))
                    if b:
                        narrow.wait_full(vec, ("mT", b - 1))
                    link(v.tensor_scalar(nm[:, :, 0, :], mx[:], -1.0, None, ALU.mult))
                    v.scalar_tensor_tensor(out=nm[:, :, 1, :], in0=mx[:], scalar=-1.0, in1=nm[:, :, 0, :],
                                           op0=ALU.mult, op1=ALU.subtract).then_inc(nm_done, 1)

                def finish_pair(b, hp):
                    n = b * HP + hp
                    vec.wait_ge(pv_done, b * H + 2 * hp + 2)
                    ps = outr.slot(("out", b, hp))[:, 0:2 * TI * VW].rearrange("p (g w) -> p g w", w=VW)
                    if n:
                        vec.wait_ge(att_done, n)
                    v.tensor_reduce(red[:], ps[:, :, 0:3 * DH].rearrange("p g (r d) -> p g d r", d=DH), AX_X,
                                    ALU.add)
                    outr.taken(v.reciprocal(rden[:], ps[:, :, 3 * DH]), ("out", b, hp))
                    outr.wait_taken(vec, ("out", b, hp))
                    if hp == 0 and b:
                        wide.wait_full(vec, ("attT", b - 1))
                    for j in range(2):
                        h = 2 * hp + j
                        ins = v.tensor_tensor(att[:, :, h * DH:(h + 1) * DH], red[:, j * TI:(j + 1) * TI, :],
                                              rden[:, j * TI:(j + 1) * TI].unsqueeze(2).to_broadcast([P, TI, DH]),
                                              ALU.mult)
                    ins.then_inc(att_done, 1)

                def post(b):
                    for j in range(2):
                        ps = narrow.wait_full(vec, ("proj", b, j))
                        t = xs[:, b * TI + 2 * j:b * TI + 2 * j + 2, :]
                        narrow.taken(v.tensor_tensor(t, t, ps.rearrange("p (i d) -> p i d", d=D), ALU.add),
                                     ("proj", b, j))
                    for j in range(2):
                        narrow.wait_taken(vec, ("proj", b, j))
                    if b:
                        vec.wait_ge(rows_stored, 16 * b)
                    normalise(xs[:, b * TI:(b + 1) * TI, :], xw, norm2_done)
                    narrow.wait_taken(vec, ("router", b))
                    for i in range(TI):
                        ins = v.max(lv[:, i, E:E + K], lv[:, i, 0:E])
                    link(ins)
                    for i in range(TI):
                        ins = v.match_replace(lrep[:, i, :], lv[:, i, E:E + K], lv[:, i, 0:E], -3e38)
                    link(ins)
                    if b:
                        link(v.tensor_copy(before[:, 0, :], before[:, TI, :]))
                    link(v.tensor_tensor(chosen[:], lrep[:], lv[:, :, 0:E], ALU.not_equal))
                    for i in range(TI):
                        ins = v.tensor_tensor(before[:, i + 1, :], before[:, i, :], chosen[:, i, :], ALU.add)
                        if i < TI - 1:
                            link(ins)
                    ins.then_inc(chosen_done, 1)
                    link(v.tensor_copy(wsum[:], lv[:, :, E]))
                    v.tensor_tensor(lv[:], lv[:], wsum[:].unsqueeze(2).to_broadcast([P, TI, E + K]),
                                    ALU.subtract).then_inc(lvs_done, 1)
                    vec.wait_ge(ev_done, b + 1)
                    link(v.tensor_reduce(wsum[:], ev[:, :, E:E + K], AX_X, ALU.add))
                    link(v.reciprocal(wsum[:], wsum[:]))
                    v.tensor_tensor(xw[:, :, D:XW], ev[:, :, 0:E], wsum[:].unsqueeze(2).to_broadcast([P, TI, E]),
                                    ALU.mult).then_inc(xw_done, 1)
                    ps = narrow.wait_full(vec, ("count", b))
                    narrow.taken(v.tensor_tensor(comp[:], ps[:, 0:TI * E].rearrange("p (i e) -> p i e", e=E),
                                                 consts[:, C_EO:C_EO + E].unsqueeze(1).to_broadcast([P, TI, E]),
                                                 ALU.add), ("count", b))
                    narrow.wait_taken(vec, ("count", b))
                    link(v.tensor_tensor(comp[:], comp[:], chosen[:], ALU.mult))
                    for i in range(TI):
                        ins = v.max(comp8[:, i, :], comp[:, i, :])
                    link(ins)
                    link(v.tensor_copy(compi[:], comp8[:].rearrange("p i k -> p (i k)")))
                    v.tensor_scalar(eki[:, 0, :], compi[:], ESH, None, ALU.logical_shift_right)
                    link(v.tensor_scalar(eki[:, 1, :], compi[:], 2 ** ESH - 1, None, ALU.bitwise_and))
                    link(v.tensor_copy(ekf[:], eki[:]))
                    vec.wait_ge(part3, 4 * min(b + 2, NB))
                    n = TI * K
                    v.tensor_tensor(ohc[:], consts[:, C_IO:C_IO + P].unsqueeze(1).to_broadcast([P, n, P]),
                                    ekf[:, 1, :].unsqueeze(2).to_broadcast([P, n, P]), ALU.is_equal)
                    link(v.tensor_tensor(ohe[:], consts[:, C_IE:C_IE + E].unsqueeze(1).to_broadcast([P, n, E]),
                                         ekf[:, 0, :].unsqueeze(2).to_broadcast([P, n, E]), ALU.is_equal))
                    for i in range(TI):
                        t = C_TOK + b * TI + i
                        ins = v.tensor_scalar(oht[:, i * K:(i + 1) * K, :], ohe[:, i * K:(i + 1) * K, :],
                                              consts[:, t:t + 1], None, ALU.mult)
                    ins.then_inc(onehot_done, 1)
                    ps = narrow.wait_full(vec, ("table", b))
                    narrow.taken(v.tensor_tensor(table[:], table[:], ps[:, 0:E], ALU.add), ("table", b))
                    narrow.wait_taken(vec, ("table", b))

                vec.wait_ge(half_set, 3)
                for step, b in schedule():
                    if step == "prep":
                        prep(b)
                    if step == "rowmax":
                        for hp in range(HP):
                            for i in range(TI):
                                row_max(b, hp, i)
                        negate_max(b)
                    if step == "attend":
                        for h in range(H):
                            if b + 1 < NB:
                                for i in range(2):
                                    row_max(b + 1, h // 2, 2 * (h % 2) + i)
                            if not on_pool(h):
                                second_part(v, vec, b, h, p2_dve)
                            if h % 2 == 1 and h > 1:
                                finish_pair(b, h // 2 - 1)
                        if b + 1 < NB:
                            negate_max(b + 1)
                        finish_pair(b, HP - 1)
                    if step == "post":
                        post(b)
                v.tensor_scalar(rows_of[:, :, 0], table[:], -1.0, 0.0, ALU.add, ALU.max)
                link(v.tensor_scalar(comp[:, 0, :], table[:], 0.0, consts[:, C_DUM:C_DUM + 1], ALU.is_equal, ALU.mult))
                v.scalar_tensor_tensor(out=rows_of[:, :, 1], in0=table[:], scalar=-1.0, in1=comp[:, 0, :],
                                       op0=ALU.add, op1=ALU.add).then_inc(rows_done, 1)


def experts(nc, xw_d, acc_d, banks, idf, rows_of, gup_v, dnp_v, out):
    ctx = ExitStack()
    with ctx:
        def sb(name, shape, dt):
            return ctx.enter_context(nc.sbuf_tensor(name, shape, dt))

        def sem(name):
            return ctx.enter_context(nc.semaphore(name))

        gup_sb = sb("gup_sb", [P, U, 2, 2 * I], F32)
        dnp_sb = sb("dnp_sb", [I, U, D], F32)
        gath = sb("gath", [P, U, XW], F32)
        xTe = sb("xTe", [P, 2, DC, P], F32)
        gate = sb("gate", [I, 2, P], F32)
        hid = sb("hid", [I, 2, P], F32)
        wcol = sb("wcol", [P, U], F32)
        ye = sb("ye", [P, U, D], F32)
        total = sb("total", [P, NACC, NT * D], F32)
        psX = [banks[:, n, 0:DC * P].rearrange("p (c n) -> p c n", c=DC) for n in (0, 1)]
        psG = [banks[0:I, n, 0:2 * P].rearrange("p (c n) -> p c n", c=2) for n in (2, 3)]
        psY = [banks[:, n, 0:D] for n in (4, 5)]

        gup_in = [sem(f"gup_in{h}") for h in range(2)]
        dnp_in = [sem(f"dnp_in{h}") for h in range(2)]
        gath_in = [sem(f"gath_in{s}") for s in range(U)]
        x_turned, x_copied = sem("x_turned"), sem("x_copied")
        gu_done, gate_done, hid_done = sem("gu_done"), sem("gate_done"), sem("hid_done")
        down_done, cols_done, y_done = sem("down_done"), sem("cols_done"), sem("y_done")
        added = [sem(f"added{a}") for a in range(NACC)]
        total_in = [sem(f"total_in{c}") for c in range(NB)]
        sum_done, out_set = sem("sum_done"), sem("out_set")

        def wait(eng, s, value):
            if not isinstance(value, int) or value > 0:
                eng.wait_ge(s, value)

        def rounds(eng, body):
            body(0, False)
            with eng.Fori(1, NR - 1) as k:
                body(k, False)
            body(NR - 1, True)

        CW = NT * D // NB

        with nc.Block() as block:
            @block.sync
            def _(sp):
                for h in range(2):
                    o = h * U // 2
                    sp.dma_start(gup_sb[:, o:o + U // 2], gup_v[:, o:o + U // 2]).then_inc(gup_in[h], 16)
                    sp.dma_start(dnp_sb[:, o:o + U // 2], dnp_v[:, o:o + U // 2]).then_inc(dnp_in[h], 16)

                def body(k, last):
                    if last:
                        return
                    for h in range(2):
                        sp.wait_ge(down_done, k * U + (h + 1) * U // 2)
                        o = h * U // 2
                        e = bass.ds((k + 1) * U + o, U // 2)
                        sp.dma_start(gup_sb[:, o:o + U // 2], gup_v[:, e]).then_inc(gup_in[h], 16)
                        sp.dma_start(dnp_sb[:, o:o + U // 2], dnp_v[:, e]).then_inc(dnp_in[h], 16)

                rounds(sp, body)
                for a in range(NACC):
                    sp.wait_ge(added[a], 16 * (E // NACC))
                for c in range(NB):
                    for a in range(NACC):
                        sp.dma_start(total[:, a, c * CW:(c + 1) * CW],
                                     acc_d[a][0:NTOK, :].rearrange("(p r) d -> p (r d)", p=P)[:, c * CW:(c + 1) * CW]
                                     ).then_inc(total_in[c], 16)
                for c in range(NB):
                    sp.wait_ge(sum_done, (NACC - 1) * (c + 1))
                    sp.dma_start(out.rearrange("(p r) d -> p (r d)", p=P)[:, c * CW:(c + 1) * CW],
                                 total[:, 0, c * CW:(c + 1) * CW]).then_inc(out_set, 16)
                sp.wait_ge(out_set, 16 * NB)

            @block.gpsimd
            def _(pool):
                last_row = nc.gpsimd.to_reg(NTOK - 1)
                last_acc = nc.gpsimd.to_reg(ROWS - 1)

                def gather(n):
                    nc.gpsimd.indirect_dma_start(
                        out=gath[:, n % U, :], out_offset=None, in_=xw_d,
                        in_offset=bass.IndirectOffsetOnAxis(ap=rows_of[:, n, 0:1], axis=0),
                        bounds_check=last_row, oob_is_err=False).then_inc(gath_in[n % U], 16)

                for n in range(U):
                    gather(n)
                for n in range(E):
                    a = n % NACC
                    pool.wait_ge(y_done, n + 1)
                    if n >= NACC:
                        pool.wait_ge(added[a], 16 * (n // NACC))
                    nc.gpsimd.indirect_dma_start(
                        out=acc_d[a], out_offset=bass.IndirectOffsetOnAxis(ap=rows_of[:, n, 1:2], axis=0),
                        in_=ye[:, n % U, :], in_offset=None,
                        bounds_check=last_acc, oob_is_err=True, compute_op=ALU.add).then_inc(added[a], 16)
                    if n + U < E:
                        gather(n + U)

            @block.scalar
            def _(act):
                def copy_x(n, s):
                    act.wait_ge(x_turned, n + 1)
                    wait(act, gu_done, n - 1)
                    nc.scalar.copy(xTe[:, s % 2], psX[s % 2]).then_inc(x_copied, 1)

                def silu(n, s):
                    act.wait_ge(gu_done, n + 1)
                    wait(act, hid_done, n - 1)
                    nc.scalar.activation(gate[:, s % 2], psG[s % 2][:, 0], ACT.Silu).then_inc(gate_done, 1)

                copy_x(0, 0)
                copy_x(1, 1)
                silu(0, 0)

                def body(k, last):
                    for s in range(U):
                        n = k * U + s
                        if not last or s + 2 < U:
                            copy_x(n + 2, s)
                        if not last or s + 1 < U:
                            silu(n + 1, s + 1)

                rounds(act, body)

            @block.tensor
            def _(pe):
                def turn(n, s, k):
                    pe.wait_ge(gath_in[s % U], 16 * (k + s // U + 1))
                    wait(pe, x_copied, n - 1)
                    rows = gath[:, s % U, 0:D].rearrange("p (n c) -> p c n", c=DC)
                    for c in range(DC):
                        ins = nc.tensor.transpose(psX[s % 2][:, c, :], rows[:, c, :], idf)
                    ins.then_inc(x_turned, 1)

                def gate_up(n, s, k):
                    pe.wait_ge(x_copied, n + 1)
                    if s % (U // 2) == 0:
                        pe.wait_ge(gup_in[s % U // (U // 2)], 16 * (k + s // U + 1))
                    wait(pe, hid_done, n - 1)
                    for r in range(2):
                        for c in range(DC):
                            ins = nc.tensor.matmul(psG[s % 2][:, r, :], gup_sb[:, s % U, c, r * I:(r + 1) * I],
                                                   xTe[:, s % 2, c, :], start=(c == 0), stop=(c == DC - 1))
                    ins.then_inc(gu_done, 1)

                def down(n, s, k):
                    pe.wait_ge(hid_done, n + 1)
                    if s % (U // 2) == 0:
                        pe.wait_ge(dnp_in[s // (U // 2)], 16 * (k + 1))
                    wait(pe, y_done, n - 1)
                    nc.tensor.matmul(psY[s % 2], hid[:, s % 2, :], dnp_sb[:, s, :], start=True,
                                     stop=True).then_inc(down_done, 1)

                turn(0, 0, 0)
                turn(1, 1, 0)
                gate_up(0, 0, 0)

                def body(k, last):
                    for s in range(U):
                        n = k * U + s
                        if not last or s + 2 < U:
                            turn(n + 2, s + 2, k)
                        if not last or s + 1 < U:
                            gate_up(n + 1, s + 1, k)
                        down(n, s, k)

                rounds(pe, body)

            @block.vector
            def _(vec):
                v = nc.vector

                def hidden(n, s):
                    vec.wait_ge(gate_done, n + 1)
                    wait(vec, down_done, n - 1)
                    v.tensor_tensor(hid[:, s % 2], gate[:, s % 2], psG[s % 2][:, 1], ALU.mult).then_inc(hid_done, 1)

                def weigh(n, s, k):
                    if not isinstance(k, int) or k > 0:
                        vec.wait_ge(added[s % NACC], 16 * ((k - 1) * (U // NACC) + s // NACC + 1))
                    vec.wait_ge(gath_in[s], 16 * (k + 1))
                    v.tensor_copy(wcol[:, s:s + 1], gath[:, s, bass.ds(n + D, 1)]).then_inc(cols_done, 1)
                    vec.wait_ge(down_done, n + 1)
                    vec.wait_ge(cols_done, n + 1)
                    v.tensor_scalar(ye[:, s, :], psY[s % 2], wcol[:, s:s + 1], None, ALU.mult).then_inc(y_done, 1)

                hidden(0, 0)

                def body(k, last):
                    for s in range(U):
                        n = k * U + s
                        if not last or s + 1 < U:
                            hidden(n + 1, s + 1)
                        weigh(n, s, k)

                rounds(vec, body)
                for c in range(NB):
                    vec.wait_ge(total_in[c], 16 * NACC)
                    t = total[:, :, c * CW:(c + 1) * CW]
                    for a in range(1, NACC):
                        if a > 1:
                            vec.wait_ge(sum_done, (NACC - 1) * c + a - 1)
                        v.tensor_tensor(t[:, 0, :], t[:, 0, :], t[:, a, :], ALU.add).then_inc(sum_done, 1)


def kernel(**inputs):
    import concourse.bacc as _bacc
    from concourse.bass_utils import run_bass_kernel_spmd as _run

    x = np.asarray(inputs["L0_attn_x"])
    w = np.asarray(inputs["L0_attn_w_qkv"])
    swap = np.arange(2 * D).reshape(-1, 2, DH // 2)[:, ::-1].reshape(-1)
    wt = w.T
    cst, rot = constants()
    arrays = {
        "in_x": np.ascontiguousarray(x.reshape(NTOK, D)),
        "in_wqk": np.ascontiguousarray(np.concatenate([wt[:, :2 * D], wt[:, :2 * D][:, swap]], 1)),
        "in_wv": np.ascontiguousarray(wt[:, 2 * D:]),
        "in_wp": np.ascontiguousarray(np.asarray(inputs["L0_attn_w_proj"]).T),
        "in_wr": np.ascontiguousarray(np.asarray(inputs["L0_ffn_router_weight"]).T),
        "in_gup": np.ascontiguousarray(inputs["L0_ffn_gate_up_proj"]),
        "in_dnp": np.ascontiguousarray(inputs["L0_ffn_down_proj"]),
        "in_cst": cst,
        "in_rot": rot,
    }
    nc = _bacc.Bacc("TRN2", target_bir_lowering=False, num_devices=1)
    args = [nc.dram_tensor(n, a.shape, mybir.dt.from_np(a.dtype), kind="ExternalInput").ap()
            for n, a in arrays.items()]
    args.append(nc.dram_tensor("out_y", (NTOK, D), F32, kind="ExternalOutput").ap())
    build(nc, *args)
    r = _run(nc, [arrays], core_ids=[0])
    return r.results[0]["out_y"].reshape(x.shape)
```

```python
from contextlib import ExitStack

import numpy as np

import concourse.bass as bass
from concourse import mybir

F32 = mybir.dt.float32
BF16 = mybir.dt.bfloat16
F16 = mybir.dt.float16
I32 = mybir.dt.int32
U32 = mybir.dt.uint32
ALU = mybir.AluOpType
ACT = mybir.ActivationFunctionType
AX_X = mybir.AxisListType.X

P = 128
NB, T, D = 4, 512, 256
H, DH = 16, 16
E, I, K, CAP = 64, 96, 8, 128
TI = T // P
NT = NB * TI
NTOK = NB * T
HP = H // 2
DC = D // P
SCALE = DH ** -0.5
EPS = 1e-5
MASKED = -1e30
PAIRS_Q = (0, 0, 1, 1, 0, 2)
PAIRS_K = (0, 1, 0, 1, 2, 0)
SR = len(PAIRS_Q) * DH
VW = 3 * DH + 1
POFF = (0, 512, 896, 1152)
PW = 1280
GROUPS = ((0,), (1,), (2, 3))
XW = D + E
NACC = 2
ROWS = NTOK + P
U = 8
NR = E // U
NCLR = 4
NSET = (NCLR + 1) * (NACC - 1) + 1
ESH = 12

MAX_FROM, MAX_EACH = 3, 3
POST_AT = (0, 1, 2, 4, 5, 6, 8, 9, 10, 11, 12, 13, 14, 15)
PREP_AT = (0, 3, 4, 5, 6, 7, 8, 9, 10, 11)

C_ID, C_MQ, C_MK, C_TRI, C_IO, C_EO, C_IE, C_TOK, C_DUM, C_ONE = 0, 128, 256, 384, 512, 640, 704, 768, 784, 785
NCONST = C_ONE + P


def constants():
    c = np.zeros((P, NCONST), np.float32)
    r, q = np.arange(P)[:, None], np.arange(P)[None, :]
    c[:, C_ID:C_ID + P] = r == q
    c[:, C_MQ:C_MQ + P] = np.where(q > r, MASKED, 0)
    c[:, C_MK:C_MK + P] = np.where(r > q, MASKED, 0)
    c[:, C_TRI:C_TRI + P] = r <= q
    c[:, C_IO:C_IO + P] = q + 1
    c[:, C_EO:C_EO + E] = np.arange(E) * 2.0 ** ESH
    c[:, C_IE:C_IE + E] = np.arange(E)
    c[:, C_TOK:C_TOK + NT] = r + 1 + P * np.arange(NT)
    c[:, C_DUM:C_DUM + 1] = NTOK + 1 + r
    c[:, C_ONE:] = 1.0
    inv = (1.0 / np.float32(10000.0) ** (np.arange(0, DH, 2, dtype=np.float32) / np.float32(DH))).astype(np.float32)
    f = np.outer(np.arange(T, dtype=np.float32), inv).astype(np.float32)
    emb = np.concatenate([f, f], -1)
    cos, sin = np.cos(emb).T, np.sin(emb).T
    sin = np.concatenate([-sin[:DH // 2], sin[DH // 2:]], 0)
    rot = np.stack([np.tile(cos, (P // DH, 1)), np.tile(sin, (P // DH, 1))], 1).astype(np.float32)
    return c, rot


def prep_stages(b):
    stages = [[("norm1", b)], [("xnT", b)]]
    for n in range(7):
        st = []
        for kind, lag in (("third", 3), ("resid", 2), ("rope", 0), ("sum", 1)):
            if 0 <= n - lag < 4:
                st.append((kind, b, n - lag))
        stages.append(st)
    return stages + [[("store", b)]]


def post_stages(b):
    return [
        [("attT", b)],
        [("proj", b, 0), ("proj", b, 1)],
        [("norm2", b)],
        [("x2T", b)],
        [("router", b)],
        [("top", b)],
        [("count", b)],
        [("weights", b)],
        [("choice", b)],
        [("onehot", b, 0)],
        [("onehot", b, 1)],
        [("onehot", b, 2)],
        [("onehot", b, 3)],
        [("table", b)],
    ]


def plan():
    order = []
    for st in prep_stages(0):
        order += st
    order += [("load", 0), ("ones",), ("v", 0, 0), ("v", 0, 1), ("vrest", 0, 0), ("vrest", 0, 1)]
    for st in prep_stages(1):
        order += st
    order.append(("load", 1))
    order += [("max", 0, hp, i) for hp in range(HP) for i in range(TI)] + [("negate", 0), ("mT", 0)]
    for b in range(NB):
        extras = [[] for _ in range(H)]
        if b + 1 < NB:
            extras[0] += [("v", b + 1, 0)]
            extras[1] += [("v", b + 1, 1), ("vrest", b + 1, 0)]
            extras[2] += [("vrest", b + 1, 1)]
        if b >= 1:
            for st, h in zip(post_stages(b - 1), POST_AT):
                extras[h] += st
        if b + 2 < NB:
            for st, h in zip(prep_stages(b + 2), PREP_AT):
                extras[h] += st
        maxima = [("max", b + 1, hp, i) for hp in range(HP) for i in range(TI)] if b + 1 < NB else []
        for h in range(H):
            now = []
            if MAX_FROM <= h:
                now, maxima = maxima[:MAX_EACH], maxima[MAX_EACH:]
            if h % 2 == 1 and h > 1:
                order.append(("finish", b, h // 2 - 1))
            order.append(("s", b, h, 0))
            order += now[0:1]
            if h:
                order.append(("second", b, h - 1))
            order.append(("s", b, h, 1))
            order += now[1:2] + extras[h]
            order.append(("s", b, h, 2))
            order += now[2:]
            if h:
                order.append(("pv", b, h - 1))
            if now and not maxima:
                order.append(("negate", b + 1))
                ended = h
            if b + 1 < NB and not maxima and h == ended + 1:
                order.append(("mT", b + 1))
        order += [("second", b, H - 1), ("pv", b, H - 1), ("finish", b, HP - 1)]
        if b + 2 < NB:
            order.append(("load", b + 2))
        if b == 0:
            order.append(("clear",))
    for st in post_stages(NB - 1):
        order += st
    return order


PLAN = plan()


def ring_uses():
    wide = [p for p in PLAN if p[0] in ("xnT", "rope", "max", "attT", "x2T")]
    narrow = [p for p in PLAN if p[0] in ("v", "mT", "s", "proj", "router", "count", "table")]
    out = [("out", b, hp) for b in range(NB) for hp in range(HP)]
    return [{key: n for n, key in enumerate(uses)} for uses in (wide, narrow, out)]


class Ring:

    def __init__(self, uses, slots, full, empty):
        self.uses, self.slots, self.full, self.empty = uses, slots, full, empty

    def slot(self, key):
        return self.slots[self.uses[key] % 2]

    def acquire(self, pe, key):
        n = self.uses[key]
        if n >= 2:
            pe.wait_ge(self.empty[n % 2], n // 2)
        return self.slot(key)

    def filled(self, ins, key):
        ins.then_inc(self.full[self.uses[key] % 2], 1)

    def wait_full(self, eng, key):
        n = self.uses[key]
        eng.wait_ge(self.full[n % 2], n // 2 + 1)
        return self.slot(key)

    def taken(self, ins, key):
        ins.then_inc(self.empty[self.uses[key] % 2], 1)

    def wait_taken(self, eng, key):
        n = self.uses[key]
        eng.wait_ge(self.empty[n % 2], n // 2 + 1)


def on_pool(h):
    return h % 2 == 1


def build(nc, x, wqk, wv, wp, wr, gup, dnp, cst, rot, out):
    qk_d = [nc.dram_tensor(f"qk_parts{s}", (3, 2 * D, T), BF16, kind="Internal").ap() for s in range(2)]
    m_d = [nc.dram_tensor(f"neg_max{s}", (2 * H, T), BF16, kind="Internal").ap() for s in range(2)]
    ones_d = nc.dram_tensor("ones", (P, P), BF16, kind="Internal").ap()
    xw_d = nc.dram_tensor("token_rows", (NTOK, XW), F32, kind="Internal").ap()
    acc_d = [nc.dram_tensor(f"acc{s}", (ROWS, D), F32, kind="Internal").ap() for s in range(NACC)]

    top = ExitStack()
    with top:
        def keep_sb(name, shape, dt):
            return top.enter_context(nc.sbuf_tensor(name, shape, dt))

        def sem(name):
            return top.enter_context(nc.semaphore(name))

        banks = top.enter_context(nc.psum_tensor("banks", [P, 8, 512], F32))
        consts = keep_sb("consts", [P, NCONST], F32)
        idf = consts[:, C_ID:C_ID + P]
        table = keep_sb("table", [P, E], F32)
        rows_of = keep_sb("rows_of", [P, E, 2], U32)
        const_in = sem("const_in")
        rows_stored = sem("rows_stored")
        acc_set = sem("acc_set")
        rows_done = sem("rows_done")

        gup_v = gup.rearrange("e (p c) f -> p e c f", c=DC)
        dnp_v = dnp.rearrange("e i d -> i e d")

        attention(nc, x, wqk, wv, wp, wr, cst, rot, qk_d, m_d, ones_d, xw_d, acc_d, banks, consts, table, rows_of,
                  const_in, rows_stored, acc_set, rows_done)
        experts(nc, xw_d, acc_d, banks, idf, rows_of, gup_v, dnp_v, out)


def attention(nc, x, wqk, wv, wp, wr, cst, rot, qk_d, m_d, ones_d, xw_d, acc_d, banks, consts, table, rows_of,
              const_in, rows_stored, acc_set, rows_done):
    ctx = ExitStack()
    with ctx:
        def sb(name, shape, dt):
            return ctx.enter_context(nc.sbuf_tensor(name, shape, dt))

        def sem(name):
            return ctx.enter_context(nc.semaphore(name))

        idf = consts[:, C_ID:C_ID + P]
        cb = sb("consts_bf16", [P, NCONST], BF16)
        rot_sb = sb("rot_sb", [P, 2, T], F32)
        wqk_sb = sb("wqk_sb", [P, DC, 4 * D], F32)
        wv_sb = sb("wv_sb", [P, DC, D], F32)
        wp_sb = sb("wp_sb", [P, DC, D], F32)
        wr_sb = sb("wr_sb", [P, DC, E], F32)
        xs = sb("xs", [P, NT, D], F32)
        xn = sb("xn", [P, TI, D], F32)
        xT = sb("xT", [P, DC, T], F32)
        stats = sb("stats", [P, TI, 6], F32)
        mv = sb("mv", [P, TI, 2], F32)
        vpe = sb("vpe", [P, TI], F32)
        half = sb("half", [P, TI], F32)
        rstd = sb("rstd", [P, TI], F32)
        work = sb("work", [P, 8 * T], F32)
        rc = work[:, 0:4 * T].rearrange("p (s r t) -> p s r t", s=2, r=2)
        qk = work[:, 4 * T:6 * T].rearrange("p (s t) -> p s t", s=2)
        resid = work[:, 6 * T:8 * T].rearrange("p (s t) -> p s t", s=2)
        ohc = work[:, 0:4 * T].bitcast(F16).rearrange("p (n c) -> p n c", c=CAP)
        ohe = work[:, 4 * T:6 * T].bitcast(F16).rearrange("p (n e) -> p n e", e=E)
        oht = work[:, 6 * T:8 * T].bitcast(F16).rearrange("p (n e) -> p n e", e=E)
        parts = sb("parts", [P, 3, 4, T], BF16)
        stq = [sb(f"stq{s}", [SR + 2, H, T], BF16) for s in range(2)]
        stk = [sb(f"stk{s}", [SR + 2, H, T], BF16) for s in range(2)]
        vst = [sb(f"vst{s}", [P, TI, H, VW], BF16) for s in range(2)]
        vres = sb("vres", [P, 2, 2, D], F32)
        mx = sb("mx", [P, TI, H], F32)
        nm = sb("nm", [P, TI, 2, H], BF16)
        mT = sb("mT", [2 * H, T], BF16)
        prob = sb("prob", [P, 3, PW], F32)
        prob2 = sb("prob2", [P, 3, PW], BF16)
        red = sb("red", [P, 2 * TI, DH], F32)
        rden = sb("rden", [P, 2 * TI], F32)
        att = sb("att", [P, TI, D], F32)
        attT = sb("attT", [P, DC, T], F32)
        xw = sb("xw", [P, TI, XW], F32)
        lv = sb("lv", [P, TI, E + K], F32)
        lrep = sb("lrep", [P, TI, E], F32)
        ev = sb("ev", [P, TI, E + K], F32)
        wsum = sb("wsum", [P, TI], F32)
        chosen = sb("chosen", [P, TI, E], BF16)
        before = sb("before", [P, TI + 1, E], BF16)
        comp = sb("comp", [P, TI, E], F32)
        comp8 = sb("comp8", [P, TI, K], F32)
        compi = sb("compi", [P, TI * K], I32)
        eki = sb("eki", [P, 2, TI * K], I32)
        ekf = sb("ekf", [P, 2, TI * K], F32)

        wide_uses, narrow_uses, out_uses = ring_uses()

        def ring(name, uses, slots):
            return Ring(uses, slots, [sem(f"{name}_full{s}") for s in range(2)],
                        [sem(f"{name}_empty{s}") for s in range(2)])

        wide = ring("wide", wide_uses, [banks[:, 0:2, :], banks[:, 2:4, :]])
        narrow = ring("narrow", narrow_uses, [banks[:, 4, :], banks[:, 5, :]])
        outr = ring("out", out_uses, [banks[:, 6, :], banks[:, 7, :]])

        x_in, w_in = sem("x_in"), sem("w_in")
        cast_done, ones_set, half_set = sem("cast_done"), sem("ones_set"), sem("half_set")
        stats_done, var_done, eps_done, rstd_done, norm_done = (
            sem("stats_done"), sem("var_done"), sem("eps_done"), sem("rstd_done"), sem("norm_done"))
        summed, part1, residual, part2, part3 = (
            sem("summed"), sem("part1"), sem("residual"), sem("part2"), sem("part3"))
        v1_done, v2_done, v3_done = sem("v1_done"), sem("v2_done"), sem("v3_done")
        stored = sem("stored")
        loaded = [sem(f"loaded{s}") for s in range(2)]
        nm_done, m_stored = sem("nm_done"), sem("m_stored")
        m_loaded = [sem(f"m_loaded{s}") for s in range(2)]
        p2_dve, p2_pool, pv_done = sem("p2_dve"), sem("p2_pool"), sem("pv_done")
        att_done = sem("att_done")
        norm2_done = sem("norm2_done")
        dve = sem("dve_step")
        xw_done, ev_done, lvs_done = sem("xw_done"), sem("ev_done"), sem("lvs_done")
        chosen_done, onehot_done = sem("chosen_done"), sem("onehot_done")
        zero_set, ones_stored, ones_loaded = sem("zero_set"), sem("ones_stored"), sem("ones_loaded")
        zeros = xw[:].rearrange("p i d -> p (i d)")

        maskq, maskk = cb[:, C_MQ:C_MQ + P], cb[:, C_MK:C_MK + P]
        idb, tri, onesb = cb[:, C_ID:C_ID + P], cb[:, C_TRI:C_TRI + P], cb[:, C_ONE:C_ONE + P]

        NLOAD = 2 * len(PAIRS_Q)

        def second_part(eng, queue, b, h, done):
            n = b * H + h
            narrow.wait_taken(queue, ("s", b, h, len(GROUPS) - 1))
            if n >= 3:
                queue.wait_ge(pv_done, n - 2)
            eng.tensor_tensor(prob2[:, n % 3, :], prob[:, n % 3, :], prob_lead(n % 3), ALU.subtract).then_inc(done, 1)

        def prob_lead(s):
            return prob[:, s, :].bitcast(BF16).rearrange("p (n t) -> p n t", t=2)[:, :, 1]

        with nc.Block() as block:
            @block.sync
            def _(sp):
                xv = x.rearrange("(b i p) d -> b p i d", b=NB, p=P)
                sp.dma_start(xs[:, 0:TI, :], xv[0]).then_inc(x_in, 16)
                sp.dma_start(consts[:], cst).then_inc(const_in, 16)
                sp.dma_start(wqk_sb[:], wqk.rearrange("(c p) n -> p c n", c=DC)).then_inc(w_in, 16)
                sp.dma_start(rot_sb[:], rot).then_inc(w_in, 16)
                sp.dma_start(wv_sb[:], wv.rearrange("(c p) n -> p c n", c=DC)).then_inc(w_in, 16)
                sp.dma_start(wp_sb[:], wp.rearrange("(c p) n -> p c n", c=DC)).then_inc(w_in, 16)
                sp.dma_start(wr_sb[:], wr.rearrange("(c p) n -> p c n", c=DC)).then_inc(w_in, 16)
                sp.wait_ge(x_in, 16)
                for b in range(1, NB):
                    sp.dma_start(xs[:, b * TI:(b + 1) * TI, :], xv[b]).then_inc(x_in, 16)
                for kind, *at in PLAN:
                    b = at[0] if at else 0
                    s = b % 2
                    if kind == "ones":
                        sp.wait_ge(cast_done, 1)
                        sp.dma_start(ones_d, onesb).then_inc(ones_stored, 16)
                        sp.wait_ge(ones_stored, 16)
                        for r in range(2):
                            sp.dma_start(stk[r][SR:SR + 2, :, :], ones_d.rearrange("(r g) (h t) -> r (g h t)", r=2, h=1)
                                         .rearrange("r (h t) -> r h t", t=T)).then_inc(ones_loaded, 16)
                    if kind == "clear":
                        sp.wait_ge(zero_set, 1)
                        for a in range(1, NACC):
                            rows = acc_d[a][0:NTOK, :].rearrange("(p r) d -> p (r d)", p=P)
                            for c in range(NCLR):
                                w = NT * D // NCLR
                                sp.dma_start(rows[:, c * w:(c + 1) * w], zeros[:, 0:w]).then_inc(acc_set, 16)
                            sp.dma_start(acc_d[a][NTOK:ROWS, :], zeros[:, 0:D]).then_inc(acc_set, 16)
                        sp.dma_start(acc_d[0][NTOK:ROWS, :], zeros[:, 0:D]).then_inc(acc_set, 16)
                    if kind == "store":
                        sp.wait_ge(part3, 4 * (b + 1))
                        for r in range(3):
                            sp.dma_start(qk_d[s][r].rearrange("(j p) t -> p j t", p=P),
                                         parts[:, r, :, :]).then_inc(stored, 16)
                    if kind == "load":
                        sp.wait_ge(stored, 48 * (b + 1))
                        if b >= 2:
                            narrow.wait_full(sp, ("s", b - 2, H - 1, len(GROUPS) - 1))
                        for g in range(len(PAIRS_Q)):
                            for st, pr, o in ((stq, PAIRS_Q, 0), (stk, PAIRS_K, D)):
                                src = qk_d[s][pr[g], o:o + D, :].rearrange("(h d) t -> d h t", d=DH)
                                sp.dma_start(st[s][g * DH:(g + 1) * DH, :, :], src).then_inc(loaded[s], 16)
                    if kind == "mT":
                        narrow.wait_taken(sp, ("mT", b))
                        sp.dma_start(m_d[s], mT[:]).then_inc(m_stored, 16)
                        sp.wait_ge(m_stored, 16 * (b + 1))
                        sp.dma_start(stq[s][SR:SR + 2, :, :],
                                     m_d[s].rearrange("(r h) t -> r h t", r=2)).then_inc(m_loaded[s], 16)
                    if kind == "norm2":
                        for j in range(2):
                            narrow.wait_taken(sp, ("proj", b, j))
                        sp.wait_ge(acc_set, 16 * (NSET + b))
                        sp.dma_start(acc_d[0][b * T:(b + 1) * T, :].rearrange("(i p) d -> p i d", p=P),
                                     xs[:, b * TI:(b + 1) * TI, :]).then_inc(acc_set, 16)
                    if kind == "table":
                        sp.wait_ge(xw_done, b + 1)
                        sp.dma_start(xw_d[b * T:(b + 1) * T, :].rearrange("(i p) d -> p i d", p=P),
                                     xw[:]).then_inc(rows_stored, 16)
                sp.wait_ge(rows_stored, 16 * NB)
                sp.wait_ge(acc_set, 16 * (NSET + NB))

            @block.gpsimd
            def _(pool):
                nc.gpsimd.memset(xw[:], 0.0).then_inc(zero_set, 1)
                nc.gpsimd.memset(half[:], -0.5).then_inc(half_set, 1)
                nc.gpsimd.memset(table[:], 0.0).then_inc(half_set, 1)
                nc.gpsimd.memset(before[:], 0.0).then_inc(half_set, 1)
                for s in range(2):
                    nc.gpsimd.memset(vst[s][:, :, :, 3 * DH:VW], 1.0).then_inc(ones_set, 1)
                pool.wait_ge(half_set, 3)
                norms = [0]

                def root():
                    norms[0] += 1
                    n = norms[0]
                    pool.wait_ge(var_done, n)
                    nc.gpsimd.tensor_scalar(vpe[:], mv[:, :, 1], EPS, None, ALU.add).then_inc(eps_done, 1)
                    pool.wait_ge(eps_done, n)
                    nc.gpsimd.tensor_tensor(rstd[:], vpe[:], half[:], ALU.pow).then_inc(rstd_done, 1)

                for kind, *at in PLAN:
                    b = at.pop(0) if at else None
                    if kind in ("norm1", "norm2"):
                        root()
                    if kind == "sum":
                        j, = at
                        n = 4 * b + j
                        wide.wait_taken(pool, ("rope", b, j))
                        if n >= 2:
                            pool.wait_ge(residual, n - 1)
                        nc.gpsimd.tensor_tensor(qk[:, j % 2, :], rc[:, j % 2, 0, :], rc[:, j % 2, 1, :],
                                                ALU.add).then_inc(summed, 1)
                    if kind == "resid":
                        j, = at
                        n = 4 * b + j
                        pool.wait_ge(part1, n + 1)
                        if n >= 2:
                            pool.wait_ge(part3, n - 1)
                        nc.gpsimd.tensor_tensor(resid[:, j % 2, :], qk[:, j % 2, :], parts[:, 0, j, :],
                                                ALU.subtract).then_inc(residual, 1)
                    if kind == "third":
                        j, = at
                        pool.wait_ge(part2, 4 * b + j + 1)
                        nc.gpsimd.tensor_tensor(parts[:, 2, j, :], resid[:, j % 2, :], parts[:, 1, j, :],
                                                ALU.subtract).then_inc(part3, 1)
                    if kind == "second" and on_pool(at[0]):
                        second_part(nc.gpsimd, pool, b, at[0], p2_pool)

            @block.scalar
            def _(act):
                for kind, *at in PLAN:
                    b = at.pop(0) if at else None
                    if kind == "xnT":
                        ps = wide.wait_full(act, ("xnT", b))
                        if b:
                            narrow.wait_full(act, ("v", b - 1, 1))
                        nc.scalar.copy(xT[:, 0, :], ps[:, 0, :])
                        wide.taken(nc.scalar.copy(xT[:, 1, :], ps[:, 1, :]), ("xnT", b))
                    if kind == "sum":
                        j, = at
                        if b and j == 0:
                            act.wait_ge(stored, 48 * b)
                        act.wait_ge(summed, 4 * b + j + 1)
                        nc.scalar.copy(parts[:, 0, j, :], qk[:, j % 2, :]).then_inc(part1, 1)
                    if kind == "resid":
                        j, = at
                        act.wait_ge(residual, 4 * b + j + 1)
                        nc.scalar.copy(parts[:, 1, j, :], resid[:, j % 2, :]).then_inc(part2, 1)
                    if kind == "v":
                        j, = at
                        ps = narrow.wait_full(act, ("v", b, j))
                        if b >= 2 and j == 0:
                            act.wait_ge(pv_done, H * (b - 1))
                        for i in range(2):
                            ins = nc.scalar.copy(vst[b % 2][:, 2 * j + i, :, 0:DH],
                                                 ps[:, i * D:(i + 1) * D].rearrange("p (h d) -> p h d", d=DH))
                        ins.then_inc(v1_done, 1)
                    if kind == "vrest":
                        j, = at
                        narrow.wait_taken(act, ("v", b, j))
                        for i in range(2):
                            ins = nc.scalar.copy(vst[b % 2][:, 2 * j + i, :, DH:2 * DH],
                                                 vres[:, j, i, :].rearrange("p (h d) -> p h d", d=DH))
                        ins.then_inc(v2_done, 1)
                    if kind == "s":
                        h, g = at
                        n = b * H + h
                        ps = narrow.wait_full(act, ("s", b, h, g))
                        if g == 0 and n >= 3:
                            act.wait_ge(pv_done, n - 2)
                        w = sum(T - P * j for j in GROUPS[g])
                        o = POFF[GROUPS[g][0]]
                        narrow.taken(nc.scalar.activation(prob[:, n % 3, o:o + w], ps[:, 0:w], ACT.Exp,
                                                          scale=SCALE), ("s", b, h, g))
                    if kind == "mT":
                        ps = narrow.wait_full(act, ("mT", b))
                        if b:
                            act.wait_ge(m_stored, 16 * b)
                        narrow.taken(nc.scalar.copy(mT[:], ps[0:2 * H, 0:T // 2].bitcast(BF16)), ("mT", b))
                    if kind in ("attT", "x2T"):
                        ps = wide.wait_full(act, (kind, b))
                        nc.scalar.copy(attT[:, 0, :], ps[:, 0, :])
                        wide.taken(nc.scalar.copy(attT[:, 1, :], ps[:, 1, :]), (kind, b))
                    if kind == "router":
                        ps = narrow.wait_full(act, ("router", b))
                        narrow.taken(nc.scalar.copy(lv[:, :, 0:E], ps[:, 0:TI * E].rearrange("p (i e) -> p i e", e=E)),
                                     ("router", b))
                    if kind == "weights":
                        act.wait_ge(lvs_done, b + 1)
                        nc.scalar.activation(ev[:], lv[:], ACT.Exp).then_inc(ev_done, 1)

            @block.tensor
            def _(pe):
                pe.wait_ge(cast_done, 1)

                def transposes(key, src):
                    ps = wide.acquire(pe, key)
                    for i in range(TI):
                        for c in range(DC):
                            ins = nc.tensor.transpose(ps[:, c, i * P:(i + 1) * P], src[:, i, c * P:(c + 1) * P], idf)
                    wide.filled(ins, key)

                def project(key, src, w):
                    j = key[2]
                    ps = narrow.acquire(pe, key)
                    for i in range(2):
                        for c in range(DC):
                            ins = nc.tensor.matmul(ps[:, i * D:(i + 1) * D],
                                                   src[:, c, (2 * j + i) * P:(2 * j + i + 1) * P], w[:, c, :],
                                                   start=(c == 0), stop=(c == DC - 1))
                    narrow.filled(ins, key)

                def rotate(b, j):
                    wide.wait_taken(pe, ("xnT", b))
                    if b == 0:
                        pe.wait_ge(w_in, 16 * 5)
                    ps = wide.acquire(pe, ("rope", b, j))
                    for r in range(2):
                        o = r * 2 * D + j * P
                        for c in range(DC):
                            ins = nc.tensor.matmul(ps[:, r, :], wqk_sb[:, c, o:o + P], xT[:, c, :],
                                                   start=(c == 0), stop=(c == DC - 1))
                    wide.filled(ins, ("rope", b, j))

                def row_max(b, hp, i):
                    s, w = b % 2, (i + 1) * P
                    if hp == 0 and i == 0:
                        pe.wait_ge(loaded[s], 16 * NLOAD * (b // 2 + 1))
                    ps = wide.acquire(pe, ("max", b, hp, i))
                    for j in range(2):
                        h = 2 * hp + j
                        nc.tensor.matmul(ps[:, j, i * P:w], idb, maskq, start=True, stop=False,
                                         skip_group_check=True)
                        ins = nc.tensor.matmul(ps[:, j, 0:w], stq[s][0:SR, h, i * P:w], stk[s][0:SR, h, 0:w],
                                               start=False, stop=True, skip_group_check=True)
                    wide.filled(ins, ("max", b, hp, i))

                def max_rows(b):
                    pe.wait_ge(nm_done, b + 1)
                    ps = narrow.acquire(pe, ("mT", b))[0:2 * H, 0:T // 2].bitcast(BF16)
                    for i in range(TI):
                        ins = nc.tensor.transpose(ps[:, i * P:(i + 1) * P],
                                                  nm[:, i, :, :].rearrange("p r h -> p (r h)"), idb)
                    narrow.filled(ins, ("mT", b))

                def scores(b, h, g):
                    s = b % 2
                    if h == 0 and g == 0:
                        if b == 0:
                            pe.wait_ge(ones_loaded, 32)
                        pe.wait_ge(m_loaded[s], 16 * (b // 2 + 1))
                    ps = narrow.acquire(pe, ("s", b, h, g))
                    o = 0
                    for j in GROUPS[g]:
                        w = T - j * P
                        nc.tensor.matmul(ps[:, o:o + P], idb, maskk, start=True, stop=False,
                                         skip_group_check=True)
                        ins = nc.tensor.matmul(ps[:, o:o + w], stk[s][:, h, j * P:(j + 1) * P],
                                               stq[s][:, h, j * P:T], start=False, stop=True,
                                               skip_group_check=True)
                        o += w
                    narrow.filled(ins, ("s", b, h, g))

                def attend_head(b, h):
                    n, s = b * H + h, b % 2
                    if n == 0:
                        pe.wait_ge(ones_set, 2)
                    if h == 0:
                        pe.wait_ge(v3_done, 2 * (b + 1))
                    if on_pool(h):
                        pe.wait_ge(p2_pool, n // 2 + 1)
                    else:
                        pe.wait_ge(p2_dve, n // 2 + 1)
                    key = ("out", b, h // 2)
                    ps = outr.acquire(pe, key) if h % 2 == 0 else outr.slot(key)
                    lead, rest = prob_lead(n % 3), prob2[:, n % 3, :]
                    for i in range(TI):
                        o = (h % 2 * TI + i) * VW
                        for j in range(i + 1):
                            c = POFF[j] + (i - j) * P
                            for part in (lead, rest):
                                ins = nc.tensor.matmul(ps[:, o:o + VW], part[:, c:c + P], vst[s][:, j, h, :],
                                                       start=(j == 0 and part is lead),
                                                       stop=(j == i and part is rest), skip_group_check=True)
                        if i == TI - 1:
                            ins.then_inc(pv_done, 1)

                for kind, *at in PLAN:
                    b = at.pop(0) if at else None
                    if kind == "xnT":
                        pe.wait_ge(norm_done, b + 1)
                        transposes(("xnT", b), xn)
                    if kind == "rope":
                        rotate(b, *at)
                    if kind == "v":
                        project(("v", b, *at), xT, wv_sb)
                    if kind == "max":
                        row_max(b, *at)
                    if kind == "mT":
                        max_rows(b)
                    if kind == "s":
                        scores(b, *at)
                    if kind == "pv":
                        attend_head(b, *at)
                    if kind == "attT":
                        pe.wait_ge(att_done, HP * (b + 1))
                        transposes(("attT", b), att)
                    if kind == "proj":
                        wide.wait_taken(pe, ("attT", b))
                        project(("proj", b, *at), attT, wp_sb)
                    if kind == "x2T":
                        pe.wait_ge(norm2_done, b + 1)
                        transposes(("x2T", b), xw)
                    if kind == "router":
                        wide.wait_taken(pe, ("x2T", b))
                        ps = narrow.acquire(pe, ("router", b))
                        for i in range(TI):
                            for c in range(DC):
                                ins = nc.tensor.matmul(ps[:, i * E:(i + 1) * E], attT[:, c, i * P:(i + 1) * P],
                                                       wr_sb[:, c, :], start=(c == 0), stop=(c == DC - 1))
                        narrow.filled(ins, ("router", b))
                    if kind == "count":
                        pe.wait_ge(chosen_done, b + 1)
                        ps = narrow.acquire(pe, ("count", b))
                        for i in range(TI):
                            nc.tensor.matmul(ps[:, i * E:(i + 1) * E], tri, chosen[:, i, :], start=True, stop=False)
                            ins = nc.tensor.matmul(ps[:, i * E:(i + 1) * E], onesb, before[:, i, :], start=False,
                                                   stop=True)
                        narrow.filled(ins, ("count", b))
                    if kind == "table":
                        pe.wait_ge(onehot_done, TI * (b + 1))
                        ps = narrow.acquire(pe, ("table", b))
                        for n in range(TI * K):
                            ins = nc.tensor.matmul(ps[:, 0:E], ohc[:, n, :], oht[:, n, :], start=(n == 0),
                                                   stop=(n == TI * K - 1))
                        narrow.filled(ins, ("table", b))

            @block.vector
            def _(vec):
                v = nc.vector
                step_n = [0]

                def link(ins):
                    step_n[0] += 1
                    ins.then_inc(dve, 1)
                    vec.wait_ge(dve, step_n[0])

                vec.wait_ge(const_in, 16)
                v.tensor_copy(cb[:], consts[:]).then_inc(cast_done, 1)
                norms = [0]

                def normalise(src, dst, done):
                    norms[0] += 1
                    n = norms[0]
                    for i in range(TI):
                        ins = v.bn_stats(stats[:, i, :], src[:, i, :])
                    link(ins)
                    for i in range(TI):
                        ins = v.bn_aggr(mv[:, i, :], stats[:, i, :])
                    ins.then_inc(var_done, 1)
                    vec.wait_ge(rstd_done, n)
                    for i in range(TI):
                        ins = v.tensor_scalar(dst[:, i, 0:D], src[:, i, :], mv[:, i, 0:1], rstd[:, i:i + 1],
                                              ALU.subtract, ALU.mult)
                    ins.then_inc(done, 1)

                def rotate(b, j):
                    n = 4 * b + j
                    if n == 0:
                        vec.wait_ge(w_in, 16 * 5)
                    ps = wide.wait_full(vec, ("rope", b, j))
                    if n >= 2:
                        vec.wait_ge(summed, n - 1)
                    v.tensor_tensor(rc[:, j % 2, 0, :], ps[:, 0, :], rot_sb[:, 0, :], ALU.mult)
                    wide.taken(v.tensor_tensor(rc[:, j % 2, 1, :], ps[:, 1, :], rot_sb[:, 1, :], ALU.mult),
                               ("rope", b, j))

                def value_residual(b, j):
                    n = 2 * b + j
                    vec.wait_ge(v1_done, n + 1)
                    if n >= 2:
                        vec.wait_ge(v2_done, n - 1)
                        vec.wait_ge(v3_done, n - 1)
                    ps = narrow.wait_full(vec, ("v", b, j))
                    for i in range(2):
                        ins = v.tensor_tensor(vres[:, j, i, :].rearrange("p (h d) -> p h d", d=DH),
                                              ps[:, i * D:(i + 1) * D].rearrange("p (h d) -> p h d", d=DH),
                                              vst[b % 2][:, 2 * j + i, :, 0:DH], ALU.subtract)
                    narrow.taken(ins, ("v", b, j))

                def value_third(b, j):
                    vec.wait_ge(v2_done, 2 * b + j + 1)
                    for i in range(2):
                        ins = v.tensor_tensor(vst[b % 2][:, 2 * j + i, :, 2 * DH:3 * DH],
                                              vres[:, j, i, :].rearrange("p (h d) -> p h d", d=DH),
                                              vst[b % 2][:, 2 * j + i, :, DH:2 * DH], ALU.subtract)
                    ins.then_inc(v3_done, 1)

                def row_max(b, hp, i):
                    ps = wide.wait_full(vec, ("max", b, hp, i))
                    if b and hp == 0 and i == 0:
                        vec.wait_ge(nm_done, b)
                    wide.taken(v.tensor_reduce(mx[:, i, 2 * hp:2 * hp + 2], ps[:, :, 0:(i + 1) * P], AX_X, ALU.max),
                               ("max", b, hp, i))

                def negate_max(b):
                    for i in (2, 3):
                        wide.wait_taken(vec, ("max", b, HP - 1, i))
                    if b:
                        narrow.wait_full(vec, ("mT", b - 1))
                    link(v.tensor_scalar(nm[:, :, 0, :], mx[:], -1.0, None, ALU.mult))
                    v.scalar_tensor_tensor(out=nm[:, :, 1, :], in0=mx[:], scalar=-1.0, in1=nm[:, :, 0, :],
                                           op0=ALU.mult, op1=ALU.subtract).then_inc(nm_done, 1)

                def finish_pair(b, hp):
                    n = b * HP + hp
                    vec.wait_ge(pv_done, b * H + 2 * hp + 2)
                    ps = outr.slot(("out", b, hp))[:, 0:2 * TI * VW].rearrange("p (g w) -> p g w", w=VW)
                    if n:
                        vec.wait_ge(att_done, n)
                    v.tensor_reduce(red[:], ps[:, :, 0:3 * DH].rearrange("p g (r d) -> p g d r", d=DH), AX_X,
                                    ALU.add)
                    outr.taken(v.reciprocal(rden[:], ps[:, :, 3 * DH]), ("out", b, hp))
                    outr.wait_taken(vec, ("out", b, hp))
                    if hp == 0 and b:
                        wide.wait_full(vec, ("attT", b - 1))
                    for j in range(2):
                        h = 2 * hp + j
                        ins = v.tensor_tensor(att[:, :, h * DH:(h + 1) * DH], red[:, j * TI:(j + 1) * TI, :],
                                              rden[:, j * TI:(j + 1) * TI].unsqueeze(2).to_broadcast([P, TI, DH]),
                                              ALU.mult)
                    ins.then_inc(att_done, 1)

                def top_eight(b):
                    narrow.wait_taken(vec, ("router", b))
                    for i in range(TI):
                        ins = v.max(lv[:, i, E:E + K], lv[:, i, 0:E])
                    link(ins)
                    for i in range(TI):
                        ins = v.match_replace(lrep[:, i, :], lv[:, i, E:E + K], lv[:, i, 0:E], -3e38)
                    link(ins)
                    if b:
                        link(v.tensor_copy(before[:, 0, :], before[:, TI, :]))
                    link(v.tensor_tensor(chosen[:], lrep[:], lv[:, :, 0:E], ALU.not_equal))
                    for i in range(TI):
                        ins = v.tensor_tensor(before[:, i + 1, :], before[:, i, :], chosen[:, i, :], ALU.add)
                        if i < TI - 1:
                            link(ins)
                    ins.then_inc(chosen_done, 1)
                    link(v.tensor_copy(wsum[:], lv[:, :, E]))
                    v.tensor_tensor(lv[:], lv[:], wsum[:].unsqueeze(2).to_broadcast([P, TI, E + K]),
                                    ALU.subtract).then_inc(lvs_done, 1)

                def weights(b):
                    vec.wait_ge(ev_done, b + 1)
                    link(v.tensor_reduce(wsum[:], ev[:, :, E:E + K], AX_X, ALU.add))
                    link(v.reciprocal(wsum[:], wsum[:]))
                    v.tensor_tensor(xw[:, :, D:XW], ev[:, :, 0:E], wsum[:].unsqueeze(2).to_broadcast([P, TI, E]),
                                    ALU.mult).then_inc(xw_done, 1)

                def choices(b):
                    narrow.wait_taken(vec, ("count", b))
                    link(v.tensor_tensor(comp[:], comp[:], chosen[:], ALU.mult))
                    for i in range(TI):
                        ins = v.max(comp8[:, i, :], comp[:, i, :])
                    link(ins)
                    link(v.tensor_copy(compi[:], comp8[:].rearrange("p i k -> p (i k)")))
                    v.tensor_scalar(eki[:, 0, :], compi[:], ESH, None, ALU.logical_shift_right)
                    link(v.tensor_scalar(eki[:, 1, :], compi[:], 2 ** ESH - 1, None, ALU.bitwise_and))
                    link(v.tensor_copy(ekf[:], eki[:]))

                def one_hots(b, i):
                    if i == 0:
                        vec.wait_ge(part3, 4 * min(b + 4, NB))
                    c, t = slice(i * K, (i + 1) * K), C_TOK + b * TI + i
                    v.tensor_tensor(ohc[:, c, :], consts[:, C_IO:C_IO + P].unsqueeze(1).to_broadcast([P, K, P]),
                                    ekf[:, 1, c].unsqueeze(2).to_broadcast([P, K, P]), ALU.is_equal)
                    link(v.tensor_tensor(ohe[:, c, :], consts[:, C_IE:C_IE + E].unsqueeze(1).to_broadcast([P, K, E]),
                                         ekf[:, 0, c].unsqueeze(2).to_broadcast([P, K, E]), ALU.is_equal))
                    v.tensor_scalar(oht[:, c, :], ohe[:, c, :], consts[:, t:t + 1], None,
                                    ALU.mult).then_inc(onehot_done, 1)

                vec.wait_ge(half_set, 3)
                for kind, *at in PLAN:
                    b = at.pop(0) if at else None
                    if kind == "norm1":
                        vec.wait_ge(x_in, 16 if b == 0 else 16 * NB)
                        if b:
                            wide.wait_full(vec, ("xnT", b - 1))
                        normalise(xs[:, b * TI:(b + 1) * TI, :], xn, norm_done)
                    if kind == "rope":
                        rotate(b, *at)
                    if kind == "v":
                        value_residual(b, *at)
                    if kind == "vrest":
                        value_third(b, *at)
                    if kind == "max":
                        row_max(b, *at)
                    if kind == "negate":
                        negate_max(b)
                    if kind == "second" and not on_pool(at[0]):
                        second_part(v, vec, b, at[0], p2_dve)
                    if kind == "finish":
                        finish_pair(b, *at)
                    if kind == "proj":
                        j, = at
                        ps = narrow.wait_full(vec, ("proj", b, j))
                        t = xs[:, b * TI + 2 * j:b * TI + 2 * j + 2, :]
                        narrow.taken(v.tensor_tensor(t, t, ps.rearrange("p (i d) -> p i d", d=D), ALU.add),
                                     ("proj", b, j))
                    if kind == "norm2":
                        for j in range(2):
                            narrow.wait_taken(vec, ("proj", b, j))
                        if b:
                            vec.wait_ge(rows_stored, 16 * b)
                        else:
                            vec.wait_ge(acc_set, 16 * NSET)
                        normalise(xs[:, b * TI:(b + 1) * TI, :], xw, norm2_done)
                    if kind == "top":
                        top_eight(b)
                    if kind == "count":
                        ps = narrow.wait_full(vec, ("count", b))
                        narrow.taken(v.tensor_tensor(comp[:], ps[:, 0:TI * E].rearrange("p (i e) -> p i e", e=E),
                                                         consts[:, C_EO:C_EO + E].unsqueeze(1).to_broadcast([P, TI, E]),
                                                         ALU.add), ("count", b))
                    if kind == "weights":
                        weights(b)
                    if kind == "choice":
                        choices(b)
                    if kind == "onehot":
                        one_hots(b, *at)
                    if kind == "table":
                        ps = narrow.wait_full(vec, ("table", b))
                        narrow.taken(v.tensor_tensor(table[:], table[:], ps[:, 0:E], ALU.add), ("table", b))
                        narrow.wait_taken(vec, ("table", b))
                v.tensor_scalar(rows_of[:, :, 0], table[:], -1.0, 0.0, ALU.add, ALU.max)
                link(v.tensor_scalar(comp[:, 0, :], table[:], 0.0, consts[:, C_DUM:C_DUM + 1], ALU.is_equal, ALU.mult))
                v.scalar_tensor_tensor(out=rows_of[:, :, 1], in0=table[:], scalar=-1.0, in1=comp[:, 0, :],
                                       op0=ALU.add, op1=ALU.add).then_inc(rows_done, 1)


def experts(nc, xw_d, acc_d, banks, idf, rows_of, gup_v, dnp_v, out):
    ctx = ExitStack()
    with ctx:
        def sb(name, shape, dt):
            return ctx.enter_context(nc.sbuf_tensor(name, shape, dt))

        def sem(name):
            return ctx.enter_context(nc.semaphore(name))

        gup_sb = sb("gup_sb", [P, U, 2, 2 * I], F32)
        dnp_sb = sb("dnp_sb", [I, U, D], F32)
        gath = sb("gath", [P, U, XW], F32)
        xTe = sb("xTe", [P, 2, DC, P], F32)
        gate = sb("gate", [I, 2, P], F32)
        hid = sb("hid", [I, 2, P], F32)
        wcol = sb("wcol", [P, U], F32)
        ye = sb("ye", [P, U, D], F32)
        total = sb("total", [P, NACC, NT * D], F32)
        psX = [banks[:, n, 0:DC * P].rearrange("p (c n) -> p c n", c=DC) for n in (0, 1)]
        psG = [banks[0:I, n, 0:2 * P].rearrange("p (c n) -> p c n", c=2) for n in (2, 3)]
        psY = [banks[:, n, 0:D] for n in (4, 5)]

        gup_in = [sem(f"gup_in{h}") for h in range(2)]
        dnp_in = [sem(f"dnp_in{h}") for h in range(2)]
        gath_in = [sem(f"gath_in{s}") for s in range(U)]
        x_turned, x_copied = sem("x_turned"), sem("x_copied")
        gu_done, gate_done, hid_done = sem("gu_done"), sem("gate_done"), sem("hid_done")
        down_done, cols_done, y_done = sem("down_done"), sem("cols_done"), sem("y_done")
        added = [sem(f"added{a}") for a in range(NACC)]
        total_in = [sem(f"total_in{c}") for c in range(NB)]
        sum_done, out_set = sem("sum_done"), sem("out_set")

        def wait(eng, s, value):
            if not isinstance(value, int) or value > 0:
                eng.wait_ge(s, value)

        def rounds(eng, body):
            body(0, False)
            with eng.Fori(1, NR - 1) as k:
                body(k, False)
            body(NR - 1, True)

        CW = NT * D // NB

        with nc.Block() as block:
            @block.sync
            def _(sp):
                for h in range(2):
                    o = h * U // 2
                    sp.dma_start(gup_sb[:, o:o + U // 2], gup_v[:, o:o + U // 2]).then_inc(gup_in[h], 16)
                    sp.dma_start(dnp_sb[:, o:o + U // 2], dnp_v[:, o:o + U // 2]).then_inc(dnp_in[h], 16)

                def body(k, last):
                    if last:
                        return
                    for h in range(2):
                        sp.wait_ge(down_done, k * U + (h + 1) * U // 2)
                        o = h * U // 2
                        e = bass.ds((k + 1) * U + o, U // 2)
                        sp.dma_start(gup_sb[:, o:o + U // 2], gup_v[:, e]).then_inc(gup_in[h], 16)
                        sp.dma_start(dnp_sb[:, o:o + U // 2], dnp_v[:, e]).then_inc(dnp_in[h], 16)

                rounds(sp, body)
                for a in range(NACC):
                    sp.wait_ge(added[a], 16 * (E // NACC))
                for c in range(NB):
                    for a in range(NACC):
                        sp.dma_start(total[:, a, c * CW:(c + 1) * CW],
                                     acc_d[a][0:NTOK, :].rearrange("(p r) d -> p (r d)", p=P)[:, c * CW:(c + 1) * CW]
                                     ).then_inc(total_in[c], 16)
                for c in range(NB):
                    sp.wait_ge(sum_done, (NACC - 1) * (c + 1))
                    sp.dma_start(out.rearrange("(p r) d -> p (r d)", p=P)[:, c * CW:(c + 1) * CW],
                                 total[:, 0, c * CW:(c + 1) * CW]).then_inc(out_set, 16)
                sp.wait_ge(out_set, 16 * NB)

            @block.gpsimd
            def _(pool):
                last_row = nc.gpsimd.to_reg(NTOK - 1)
                last_acc = nc.gpsimd.to_reg(ROWS - 1)

                def gather(n):
                    nc.gpsimd.indirect_dma_start(
                        out=gath[:, n % U, :], out_offset=None, in_=xw_d,
                        in_offset=bass.IndirectOffsetOnAxis(ap=rows_of[:, n, 0:1], axis=0),
                        bounds_check=last_row, oob_is_err=False).then_inc(gath_in[n % U], 16)

                for n in range(U):
                    gather(n)
                for n in range(E):
                    a = n % NACC
                    pool.wait_ge(y_done, n + 1)
                    if n >= NACC:
                        pool.wait_ge(added[a], 16 * (n // NACC))
                    nc.gpsimd.indirect_dma_start(
                        out=acc_d[a], out_offset=bass.IndirectOffsetOnAxis(ap=rows_of[:, n, 1:2], axis=0),
                        in_=ye[:, n % U, :], in_offset=None,
                        bounds_check=last_acc, oob_is_err=True, compute_op=ALU.add).then_inc(added[a], 16)
                    if n + U < E:
                        gather(n + U)

            @block.scalar
            def _(act):
                def copy_x(n, s):
                    act.wait_ge(x_turned, n + 1)
                    wait(act, gu_done, n - 1)
                    nc.scalar.copy(xTe[:, s % 2], psX[s % 2]).then_inc(x_copied, 1)

                def silu(n, s):
                    act.wait_ge(gu_done, n + 1)
                    wait(act, hid_done, n - 1)
                    nc.scalar.activation(gate[:, s % 2], psG[s % 2][:, 0], ACT.Silu).then_inc(gate_done, 1)

                copy_x(0, 0)
                copy_x(1, 1)
                silu(0, 0)

                def body(k, last):
                    for s in range(U):
                        n = k * U + s
                        if not last or s + 2 < U:
                            copy_x(n + 2, s)
                        if not last or s + 1 < U:
                            silu(n + 1, s + 1)

                rounds(act, body)

            @block.tensor
            def _(pe):
                def turn(n, s, k):
                    pe.wait_ge(gath_in[s % U], 16 * (k + s // U + 1))
                    wait(pe, x_copied, n - 1)
                    rows = gath[:, s % U, 0:D].rearrange("p (n c) -> p c n", c=DC)
                    for c in range(DC):
                        ins = nc.tensor.transpose(psX[s % 2][:, c, :], rows[:, c, :], idf)
                    ins.then_inc(x_turned, 1)

                def gate_up(n, s, k):
                    pe.wait_ge(x_copied, n + 1)
                    if s % (U // 2) == 0:
                        pe.wait_ge(gup_in[s % U // (U // 2)], 16 * (k + s // U + 1))
                    wait(pe, hid_done, n - 1)
                    for r in range(2):
                        for c in range(DC):
                            ins = nc.tensor.matmul(psG[s % 2][:, r, :], gup_sb[:, s % U, c, r * I:(r + 1) * I],
                                                   xTe[:, s % 2, c, :], start=(c == 0), stop=(c == DC - 1))
                    ins.then_inc(gu_done, 1)

                def down(n, s, k):
                    pe.wait_ge(hid_done, n + 1)
                    if s % (U // 2) == 0:
                        pe.wait_ge(dnp_in[s // (U // 2)], 16 * (k + 1))
                    wait(pe, y_done, n - 1)
                    nc.tensor.matmul(psY[s % 2], hid[:, s % 2, :], dnp_sb[:, s, :], start=True,
                                     stop=True).then_inc(down_done, 1)

                turn(0, 0, 0)
                turn(1, 1, 0)
                gate_up(0, 0, 0)

                def body(k, last):
                    for s in range(U):
                        n = k * U + s
                        if not last or s + 2 < U:
                            turn(n + 2, s + 2, k)
                        if not last or s + 1 < U:
                            gate_up(n + 1, s + 1, k)
                        down(n, s, k)

                rounds(pe, body)

            @block.vector
            def _(vec):
                v = nc.vector

                def hidden(n, s):
                    vec.wait_ge(gate_done, n + 1)
                    wait(vec, down_done, n - 1)
                    v.tensor_tensor(hid[:, s % 2], gate[:, s % 2], psG[s % 2][:, 1], ALU.mult).then_inc(hid_done, 1)

                def weigh(n, s, k):
                    if not isinstance(k, int) or k > 0:
                        vec.wait_ge(added[s % NACC], 16 * ((k - 1) * (U // NACC) + s // NACC + 1))
                    vec.wait_ge(gath_in[s], 16 * (k + 1))
                    v.tensor_copy(wcol[:, s:s + 1], gath[:, s, bass.ds(n + D, 1)]).then_inc(cols_done, 1)
                    vec.wait_ge(down_done, n + 1)
                    vec.wait_ge(cols_done, n + 1)
                    v.tensor_scalar(ye[:, s, :], psY[s % 2], wcol[:, s:s + 1], None, ALU.mult).then_inc(y_done, 1)

                hidden(0, 0)

                def body(k, last):
                    for s in range(U):
                        n = k * U + s
                        if not last or s + 1 < U:
                            hidden(n + 1, s + 1)
                        weigh(n, s, k)

                rounds(vec, body)
                for c in range(NB):
                    vec.wait_ge(total_in[c], 16 * NACC)
                    t = total[:, :, c * CW:(c + 1) * CW]
                    for a in range(1, NACC):
                        if a > 1:
                            vec.wait_ge(sum_done, (NACC - 1) * c + a - 1)
                        v.tensor_tensor(t[:, 0, :], t[:, 0, :], t[:, a, :], ALU.add).then_inc(sum_done, 1)


def kernel(**inputs):
    import concourse.bacc as _bacc
    from concourse.bass_utils import run_bass_kernel_spmd as _run

    x = np.asarray(inputs["L0_attn_x"])
    w = np.asarray(inputs["L0_attn_w_qkv"])
    swap = np.arange(2 * D).reshape(-1, 2, DH // 2)[:, ::-1].reshape(-1)
    wt = w.T
    cst, rot = constants()
    arrays = {
        "in_x": np.ascontiguousarray(x.reshape(NTOK, D)),
        "in_wqk": np.ascontiguousarray(np.concatenate([wt[:, :2 * D], wt[:, :2 * D][:, swap]], 1)),
        "in_wv": np.ascontiguousarray(wt[:, 2 * D:]),
        "in_wp": np.ascontiguousarray(np.asarray(inputs["L0_attn_w_proj"]).T),
        "in_wr": np.ascontiguousarray(np.asarray(inputs["L0_ffn_router_weight"]).T),
        "in_gup": np.ascontiguousarray(inputs["L0_ffn_gate_up_proj"]),
        "in_dnp": np.ascontiguousarray(inputs["L0_ffn_down_proj"]),
        "in_cst": cst,
        "in_rot": rot,
    }
    nc = _bacc.Bacc("TRN2", target_bir_lowering=False, num_devices=1)
    args = [nc.dram_tensor(n, a.shape, mybir.dt.from_np(a.dtype), kind="ExternalInput").ap()
            for n, a in arrays.items()]
    args.append(nc.dram_tensor("out_y", (NTOK, D), F32, kind="ExternalOutput").ap())
    build(nc, *args)
    r = _run(nc, [arrays], core_ids=[0])
    return r.results[0]["out_y"].reshape(x.shape)
```

```python
from contextlib import ExitStack

import numpy as np

import concourse.bass as bass
from concourse import mybir

F32 = mybir.dt.float32
BF16 = mybir.dt.bfloat16
F16 = mybir.dt.float16
I32 = mybir.dt.int32
U32 = mybir.dt.uint32
ALU = mybir.AluOpType
ACT = mybir.ActivationFunctionType
AX_X = mybir.AxisListType.X

P = 128
NB, T, D = 4, 512, 256
H, DH = 16, 16
E, I, K, CAP = 64, 96, 8, 128
TI = T // P
NT = NB * TI
NTOK = NB * T
HP = H // 2
DC = D // P
SCALE = DH ** -0.5
EPS = 1e-5
MASKED = -1e30
PAIRS_Q = (0, 0, 1, 1, 0, 2)
PAIRS_K = (0, 1, 0, 1, 2, 0)
SR = len(PAIRS_Q) * DH
VW = 3 * DH + 1
POFF = (0, 512, 896, 1152)
PW = 1280
MAX_PIECES = 5
GROUPS = ((0,), (1,), (2, 3))
XW = D + E
NACC = 2
ROWS = NTOK + P
WARM = 22
U = 8
NR = E // U
NCLR = 4
SUMS = 2
NSET = (NCLR + 1) * (NACC - 1) + 1
ESH = 12

NORM_AT, V_AT = 7, 9          
STAGES_FIRST = 3
MAX_BETWEEN = 2
MAX_AHEAD = 8
HALF_MAX = 2 * MAX_PIECES
MT_AFTER = 2
MT_LAG = 2
MAX_FROM = 3
MAX_EACH = (2, 2, 2, 2, 1, 1, 1, 1, 1, 1, 1, 1, 1, 1, 1, 1)
PV_LAG = 2
FIRST_HALF_AT = 13
PREP_AT = (0, 3, 4, 5, 6, 7, 8, 9, 10, 11, 12)
POST_AT = (2, 3, 4, 6, 7, 8, 9, 10, 11, 12, 13, 14, 15)
POOL_HEADS = (0, 1, 3, 4, 5, 7, 9, 10, 11, 12, 13, 14, 15)
POOL_HEADS_LAST = (1, 2, 3, 5, 7, 9, 11, 13)

C_ID, C_MQ, C_MK, C_TRI, C_IO, C_EO, C_IE, C_TOK, C_DUM, C_ONE = 0, 128, 256, 384, 512, 640, 704, 768, 784, 785
NCONST = C_ONE + P


def constants():
    c = np.zeros((P, NCONST), np.float32)
    r, q = np.arange(P)[:, None], np.arange(P)[None, :]
    c[:, C_ID:C_ID + P] = r == q
    c[:, C_MQ:C_MQ + P] = np.where(q > r, MASKED, 0)
    c[:, C_MK:C_MK + P] = np.where(r > q, MASKED, 0)
    c[:, C_TRI:C_TRI + P] = r <= q
    c[:, C_IO:C_IO + P] = q + 1
    c[:, C_EO:C_EO + E] = np.arange(E) * 2.0 ** ESH
    c[:, C_IE:C_IE + E] = np.arange(E)
    c[:, C_TOK:C_TOK + NT] = r + 1 + P * np.arange(NT)
    c[:, C_DUM:C_DUM + 1] = NTOK + 1 + r
    c[:, C_ONE:] = 1.0
    inv = (1.0 / np.float32(10000.0) ** (np.arange(0, DH, 2, dtype=np.float32) / np.float32(DH))).astype(np.float32)
    f = np.outer(np.arange(T, dtype=np.float32), inv).astype(np.float32)
    emb = np.concatenate([f, f], -1)
    cos, sin = np.cos(emb).T, np.sin(emb).T
    rot = np.stack([np.repeat(cos[:DH // 2], H, 0), np.repeat(sin[:DH // 2], H, 0)], 1).astype(np.float32)
    return c, rot


def max_blocks(g, c):
    if c < 2:
        return [(r, 0, 4 * g + 2 * c + r, 3) for r in range(2)]
    if c < 4:
        return [(r, o, 4 * g + 2 * (c - 2) + r, i) for r in range(2) for o, i in ((0, 2), (3 * P, 0))]
    return [(r, 2 * P * j, 4 * g + 2 * r + j, 1) for r in range(2) for j in range(2)]


def prep_stages(b):
    def both(kind, j):
        return [(kind, b, 2 * j), (kind, b, 2 * j + 1)]

    return [
        [("norm1", b)],
        [("xnT", b)],
        [("rope", b, 0)],
        both("sum", 0),
        [("rope", b, 1)] + both("first", 0),
        both("resid", 0) + both("sum", 1),
        both("middle", 0) + both("first", 1),
        both("third", 0) + both("resid", 1),
        [("store", b, 0)] + both("middle", 1),
        both("third", 1),
        [("store", b, 1)],
    ]


def post_stages(b):
    def pair(kind):
        return [(kind, b, 0), (kind, b, 1)]

    return [
        [("attT", b, 1)],
        [("proj", b, 1, 0), ("variance", b, 0), ("proj", b, 1, 1), ("variance", b, 1)],
        pair("norm2"),
        pair("x2T"),
        pair("router") + pair("rank"),
        [("top", b)],
        [("exps", b)],
        [("count", b), ("weights", b)],
        [("choice", b)],
        [("onehot", b, 0), ("onehot", b, 1)],
        [("onehot", b, 2), ("number", b, 0), ("onehot", b, 3), ("number", b, 1)],
        [("number", b, 2), ("number", b, 3)],
        [("table", b)],
    ]


def maxima_of(b):
    return [("max", b, g, c) for g in range(H // 4) for c in range(MAX_PIECES)]


def plan():
    order = [("ones",)]
    for n, st in enumerate(prep_stages(0)):
        order += st
        if n == NORM_AT:
            order.append(("norm1", 1))
        if n == V_AT:
            order += [("v", 0, 0), ("v", 0, 1)]
    order += [("load", 0, 0), ("load", 0, 1), ("vrest", 0, 0), ("vrest", 0, 1)]
    _, *stages = prep_stages(1)
    for _ in range(STAGES_FIRST):
        order += stages.pop(0)
    maxima = maxima_of(0)
    for n in range(HALF_MAX + MAX_AHEAD):
        order.append(maxima.pop(0))
        if n % MAX_BETWEEN == MAX_BETWEEN - 1 and stages:
            order += stages.pop(0)
        if n == HALF_MAX - 1:
            order.append(("negate", 0, 0))
        if n == HALF_MAX - 1 + MT_AFTER:
            order.append(("mT", 0, 0))
    for st in stages:
        order += st
    order += [("load", 1, 0), ("load", 1, 1)]
    due = {}
    for n in range(NB * H + PV_LAG):
        b, h = divmod(n, H)
        if h == 0 and b < NB:
            extras = [[] for _ in range(H)]
            if b + 1 < NB:
                extras[2] += [("v", b + 1, 0), ("v", b + 1, 1)]
                extras[3] += [("vrest", b + 1, 0)]
                extras[4] += [("vrest", b + 1, 1)]
            if b + 2 < NB:
                for st, at in zip(prep_stages(b + 2), PREP_AT, strict=True):
                    extras[at] += st
            if b >= 1:
                for st, at in zip(post_stages(b - 1), POST_AT, strict=True):
                    extras[at] += st
        if h == MAX_FROM and b + 1 < NB:
            maxima += maxima_of(b + 1)
        now, maxima = maxima[:MAX_EACH[h]], maxima[MAX_EACH[h]:]
        old = n - PV_LAG
        if b < NB:
            order.append(("s", b, h, 0))
        order += now[0:1]
        if 0 < n <= NB * H:
            order.append(("second", *divmod(n - 1, H)))
        if b < NB:
            order.append(("s", b, h, 1))
        order += now[1:2] + (extras[h] if b < NB else [])
        if b < NB:
            order.append(("s", b, h, 2))
        order += now[2:]
        if old >= 0:
            order.append(("pv", *divmod(old, H)))
            if old % 2 == 1:
                order.append(("finish", old // H, old % H // 2))
        for m in now:
            if m[2:] in (maxima_of(0)[HALF_MAX - 1][2:], maxima_of(0)[-1][2:]):
                half = (m[1], int(m == maxima_of(m[1])[-1]))
                order.append(("negate", *half))
                due[n + MT_LAG] = ("mT", *half)
        if n in due:
            order.append(due[n])
        if b < NB and h == FIRST_HALF_AT:
            order.append(("attT", b, 0))
        if b < NB and h == FIRST_HALF_AT + 1:
            order += [("proj", b, 0, 0), ("proj", b, 0, 1)]
        if h == H - 1 and b + 2 < NB:
            order += [("load", b + 2, 0), ("load", b + 2, 1)]
        if n == H:
            order.append(("clear",))
    for st in post_stages(NB - 1):
        order += st
    return order


PLAN = plan()


def ring_uses():
    wide = [p for p in PLAN if p[0] in ("xnT", "rope", "v", "max", "attT", "proj", "x2T", "router", "count",
                                        "table")]
    narrow = [p for p in PLAN if p[0] in ("mT", "s")]
    out = [("out", b, hp) for b in range(NB) for hp in range(HP)]
    return [{key: n for n, key in enumerate(uses)} for uses in (wide, narrow, out)]


class Ring:

    def __init__(self, uses, slots, full, empty):
        self.uses, self.slots, self.full, self.empty = uses, slots, full, empty

    def slot(self, key):
        return self.slots[self.uses[key] % 2]

    def acquire(self, pe, key):
        n = self.uses[key]
        if n >= 2:
            pe.wait_ge(self.empty[n % 2], n // 2)
        return self.slot(key)

    def filled(self, ins, key):
        ins.then_inc(self.full[self.uses[key] % 2], 1)

    def wait_full(self, eng, key):
        n = self.uses[key]
        eng.wait_ge(self.full[n % 2], n // 2 + 1)
        return self.slot(key)

    def taken(self, ins, key):
        ins.then_inc(self.empty[self.uses[key] % 2], 1)

    def wait_taken(self, eng, key):
        n = self.uses[key]
        eng.wait_ge(self.empty[n % 2], n // 2 + 1)


def on_pool(n):
    b, h = divmod(n, H)
    return h in (POOL_HEADS if b < NB - 1 else POOL_HEADS_LAST)


def shared_out(n):
    return sum(on_pool(m) == on_pool(n) for m in range(n + 1))


def build(nc, x, wqk, wv, wp, wr, gup, dnp, cst, rot, out):
    qk_d = [nc.dram_tensor(f"qk_parts{s}", (3, 2 * D, T), BF16, kind="Internal").ap() for s in range(2)]
    m_d = [nc.dram_tensor(f"neg_max{s}", (2, H, T), BF16, kind="Internal").ap() for s in range(2)]
    ones_d = nc.dram_tensor("ones", (P, P), BF16, kind="Internal").ap()
    xw_d = nc.dram_tensor("token_rows", (NTOK, XW), F32, kind="Internal").ap()
    acc_d = [out] + [nc.dram_tensor(f"acc{s}", (ROWS, D), F32, kind="Internal").ap() for s in range(1, NACC)]

    top = ExitStack()
    with top:
        def keep_sb(name, shape, dt):
            return top.enter_context(nc.sbuf_tensor(name, shape, dt))

        def sem(name):
            return top.enter_context(nc.semaphore(name))

        banks = top.enter_context(nc.psum_tensor("banks", [P, 8, 512], F32))
        consts = keep_sb("consts", [P, NCONST], F32)
        idf = consts[:, C_ID:C_ID + P]
        table = keep_sb("table", [P, E], F32)
        rows_of = keep_sb("rows_of", [P, E, 2], U32)
        const_in = sem("const_in")
        rows_stored = sem("rows_stored")
        acc_set = sem("acc_set")
        rows_done = sem("rows_done")

        gup_v = gup.rearrange("e (p c) f -> p e c f", c=DC)
        dnp_v = dnp.rearrange("e i d -> i e d")

        attention(nc, x, wqk, wv, wp, wr, cst, rot, qk_d, m_d, ones_d, xw_d, acc_d, banks, consts, table, rows_of,
                  const_in, rows_stored, acc_set, rows_done)
        experts(nc, xw_d, acc_d, banks, idf, rows_of, gup_v, dnp_v)


def attention(nc, x, wqk, wv, wp, wr, cst, rot, qk_d, m_d, ones_d, xw_d, acc_d, banks, consts, table, rows_of,
              const_in, rows_stored, acc_set, rows_done):
    ctx = ExitStack()
    with ctx:
        def sb(name, shape, dt):
            return ctx.enter_context(nc.sbuf_tensor(name, shape, dt))

        def sem(name):
            return ctx.enter_context(nc.semaphore(name))

        idf = consts[:, C_ID:C_ID + P]
        cb = sb("consts_bf16", [P, NCONST], BF16)
        rot_sb = sb("rot_sb", [P, 2, T], F32)
        wqk_sb = sb("wqk_sb", [P, DC, 2 * D], F32)
        wv_sb = sb("wv_sb", [P, DC, D], F32)
        wp_sb = sb("wp_sb", [P, DC, D], F32)
        wr_sb = sb("wr_sb", [P, DC, E], F32)
        xs = sb("xs", [P, NT, D], F32)
        xn = sb("xn", [P, TI, D], F32)
        xT = sb("xT", [P, DC, T], F32)
        stats = sb("stats", [P, TI, 6], F32)
        mv = sb("mv", [P, TI, 2], F32)
        vpe = sb("vpe", [P, TI], F32)
        half = sb("half", [P, TI], F32)
        rstd = sb("rstd", [P, TI], F32)
        stats2 = sb("stats2", [P, TI, 6], F32)
        mv2 = sb("mv2", [P, TI, 2], F32)
        vpe2 = sb("vpe2", [P, TI], F32)
        rstd2 = sb("rstd2", [P, TI], F32)
        work = sb("work", [P, 8 * T], F32)
        rc = work[:, 0:4 * T].rearrange("p (s r t) -> p s r t", s=2, r=2)
        qk = work[:, 4 * T:6 * T].rearrange("p (s t) -> p s t", s=2)
        resid = work[:, 6 * T:8 * T].rearrange("p (s t) -> p s t", s=2)
        ohc = work[:, 0:4 * T].bitcast(F16).rearrange("p (n c) -> p n c", c=CAP)
        ohe = work[:, 4 * T:6 * T].bitcast(F16).rearrange("p (n e) -> p n e", e=E)
        oht = work[:, 6 * T:8 * T].bitcast(F16).rearrange("p (n e) -> p n e", e=E)
        parts = sb("parts", [P, 3, 4, T], BF16)
        stq = [sb(f"stq{s}", [SR + 2, H, T], BF16) for s in range(2)]
        stk = [sb(f"stk{s}", [SR + 2, H, T], BF16) for s in range(2)]
        vst = [sb(f"vst{s}", [P, TI, H, VW], BF16) for s in range(2)]
        vres = sb("vres", [P, 2, 2, D], F32)
        mx = sb("mx", [P, TI, H], F32)
        nm = sb("nm", [P, TI, 2, 2, H // 2], BF16)
        mT = [sb(f"mT{f}", [H, T], BF16) for f in range(2)]
        prob = sb("prob", [P, 3, PW], F32)
        prob2 = sb("prob2", [P, 3, PW], BF16)
        red = sb("red", [P, 2 * TI, DH], F32)
        rden = sb("rden", [P, 2 * TI], F32)
        att = sb("att", [P, TI, D], F32)
        attT = sb("attT", [P, DC, T], F32)
        xw = sb("xw", [P, TI, XW], F32)
        lv = sb("lv", [P, TI, E + K], F32)
        lrep = sb("lrep", [P, TI, E], F32)
        ev = sb("ev", [P, TI, E + K], F32)
        wsum = sb("wsum", [P, TI], F32)
        chosen = sb("chosen", [P, TI, E], BF16)
        before = sb("before", [P, E], BF16)
        sum4 = sb("sum4", [P, E], F32)
        comp = sb("comp", [P, TI, E], F32)
        comp8 = sb("comp8", [P, TI, K], F32)
        compi = sb("compi", [P, TI * K], I32)
        eki = sb("eki", [P, 2, TI * K], I32)
        ekf = sb("ekf", [P, 2, TI * K], F32)

        wide_uses, narrow_uses, out_uses = ring_uses()

        def ring(name, uses, slots):
            return Ring(uses, slots, [sem(f"{name}_full{s}") for s in range(2)],
                        [sem(f"{name}_empty{s}") for s in range(2)])

        wide = ring("wide", wide_uses, [banks[:, 0:2, :], banks[:, 2:4, :]])
        narrow = ring("narrow", narrow_uses, [banks[:, 4, :], banks[:, 5, :]])
        outr = ring("out", out_uses, [banks[:, 6, :], banks[:, 7, :]])

        x_in, w_in = [sem(f"x_in{b}") for b in range(NB)], sem("w_in")
        cast_done, ones_set, half_set = sem("cast_done"), sem("ones_set"), sem("half_set")
        var_done, eps_done, rstd_done, norm_done = (
            sem("var_done"), sem("eps_done"), sem("rstd_done"), sem("norm_done"))
        summed, part1, residual, part2, part3 = (
            sem("summed"), sem("part1"), sem("residual"), sem("part2"), sem("part3"))
        v1_done, v2_done, v3_done = sem("v1_done"), sem("v2_done"), sem("v3_done")
        stored = [sem(f"stored{j}") for j in range(2)]
        loaded = [sem(f"loaded{s}") for s in range(2)]
        nm_done = [sem(f"nm_done{f}") for f in range(2)]
        m_stored = [sem(f"m_stored{f}") for f in range(2)]
        m_loaded = [[sem(f"m_loaded{s}_{f}") for f in range(2)] for s in range(2)]
        p2_dve, p2_pool, pv_done = sem("p2_dve"), sem("p2_pool"), sem("pv_done")
        att_done = sem("att_done")
        var2_done, eps2_done, rstd2_done, norm2_done = (
            sem("var2_done"), sem("eps2_done"), sem("rstd2_done"), sem("norm2_done"))
        dve = sem("dve_step")
        ranked = sem("ranked")
        xw_done, ev_done, lvs_done = sem("xw_done"), sem("ev_done"), sem("lvs_done")
        chosen_done, choices_done = sem("chosen_done"), sem("choices_done")
        ohc_done, ohe_done, oht_done = sem("slot_rows_done"), sem("expert_rows_done"), sem("token_rows_done")
        zero_set, ones_stored, ones_loaded = sem("zero_set"), sem("ones_stored"), sem("ones_loaded")
        zeros = xw[:].rearrange("p i d -> p (i d)")
        zeros_b = zeros.bitcast(BF16)

        maskq, maskk = cb[:, C_MQ:C_MQ + P], cb[:, C_MK:C_MK + P]
        idb, tri, onesb = cb[:, C_ID:C_ID + P], cb[:, C_TRI:C_TRI + P], cb[:, C_ONE:C_ONE + P]

        NLOAD = 2 * len(PAIRS_Q)

        def rotated(eng, queue, b, j):
            n = 4 * b + j
            wide.wait_taken(queue, ("rope", b, j // 2))
            if n >= 2:
                queue.wait_ge(residual, n - 1)
            eng.tensor_tensor(qk[:, j % 2, :], rc[:, 0, j % 2, :], rc[:, 1, 1 - j % 2, :],
                              ALU.add if j % 2 else ALU.subtract).then_inc(summed, 1)

        def third_part(eng, queue, b, j):
            queue.wait_ge(part2, 4 * b + j + 1)
            eng.tensor_tensor(parts[:, 2, j, :], resid[:, j % 2, :], parts[:, 1, j, :],
                              ALU.subtract).then_inc(part3, 1)

        def second_part(eng, queue, b, h, done):
            n = b * H + h
            narrow.wait_taken(queue, ("s", b, h, len(GROUPS) - 1))
            if n >= 3:
                queue.wait_ge(pv_done, n - 2)
            eng.tensor_tensor(prob2[:, n % 3, :], prob[:, n % 3, :], prob_lead(n % 3), ALU.subtract).then_inc(done, 1)

        def prob_lead(s):
            return prob[:, s, :].bitcast(BF16).rearrange("p (n t) -> p n t", t=2)[:, :, 1]

        with nc.Block() as block:
            @block.sync
            def _(sp):
                xv = x.rearrange("(b i p) d -> b p i d", b=NB, p=P)
                sp.dma_start(xs[:, 0:TI, :], xv[0]).then_inc(x_in[0], 16)
                sp.dma_start(consts[:], cst).then_inc(const_in, 16)
                sp.dma_start(wqk_sb[:], wqk.rearrange("(c p) n -> p c n", c=DC)).then_inc(w_in, 16)
                sp.dma_start(rot_sb[:], rot).then_inc(w_in, 16)
                sp.dma_start(wv_sb[:], wv.rearrange("(c p) n -> p c n", c=DC)).then_inc(w_in, 16)
                sp.dma_start(wp_sb[:], wp.rearrange("(c p) n -> p c n", c=DC)).then_inc(w_in, 16)
                sp.dma_start(wr_sb[:], wr.rearrange("(c p) n -> p c n", c=DC)).then_inc(w_in, 16)
                for b in range(1, NB):
                    sp.dma_start(xs[:, b * TI:(b + 1) * TI, :], xv[b]).then_inc(x_in[b], 16)
                for kind, *at in PLAN:
                    b = at[0] if at else 0
                    s = b % 2
                    if kind == "ones":
                        sp.wait_ge(cast_done, 1)
                        sp.dma_start(ones_d, onesb).then_inc(ones_stored, 16)
                        sp.wait_ge(ones_stored, 16)
                        for r in range(2):
                            sp.dma_start(stk[r][SR:SR + 2, :, :], ones_d.rearrange("(r g) (h t) -> r (g h t)", r=2, h=1)
                                         .rearrange("r (h t) -> r h t", t=T)).then_inc(ones_loaded, 16)
                    if kind == "clear":
                        sp.wait_ge(zero_set, 1)
                        for a in range(1, NACC):
                            rows = acc_d[a][0:NTOK, :].rearrange("(p r) d -> p (r d)", p=P)
                            for c in range(NCLR):
                                w = NT * D // NCLR
                                sp.dma_start(rows[:, c * w:(c + 1) * w], zeros[:, 0:w]).then_inc(acc_set, 16)
                            sp.dma_start(acc_d[a][NTOK:ROWS, :], zeros[:, 0:D]).then_inc(acc_set, 16)
                        sp.dma_start(acc_d[0][NTOK:ROWS, :], zeros[:, 0:D]).then_inc(acc_set, 16)
                    if kind == "store":
                        j = at[1]
                        sp.wait_ge(part3, 4 * b + 2 * j + 2)
                        for r in range(3):
                            sp.dma_start(qk_d[s][r, j * D:(j + 1) * D, :].rearrange("(j p) t -> p j t", p=P),
                                         parts[:, r, 2 * j:2 * j + 2, :]).then_inc(stored[j], 16)
                    if kind == "load":
                        j = at[1]
                        sp.wait_ge(stored[j], 48 * (b + 1))
                        if b >= 2:
                            narrow.wait_full(sp, ("s", b - 2, H - 1, len(GROUPS) - 1))
                        st, pairs = (stk, PAIRS_K) if j else (stq, PAIRS_Q)
                        for g in range(len(pairs)):
                            src = qk_d[s][pairs[g], j * D:(j + 1) * D, :].rearrange("(d h) t -> d h t", d=DH)
                            sp.dma_start(st[s][g * DH:(g + 1) * DH, :, :], src).then_inc(loaded[s], 16)
                    if kind == "mT":
                        f = at[1]
                        narrow.wait_taken(sp, ("mT", b, f))
                        rows = m_d[s].rearrange("r (f h) t -> f r h t", f=2)[f]
                        sp.dma_start(rows, mT[f][:]).then_inc(m_stored[f], 16)
                        sp.wait_ge(m_stored[f], 16 * (b + 1))
                        sp.dma_start(stq[s][SR:SR + 2, f * H // 2:(f + 1) * H // 2, :],
                                     rows).then_inc(m_loaded[s][f], 16)
                    if kind == "norm2" and at[1] == 1:
                        for j in range(2):
                            wide.wait_taken(sp, ("proj", b, 1, j))
                        sp.wait_ge(acc_set, 16 * (NSET + b))
                        sp.dma_start(acc_d[0][b * T:(b + 1) * T, :].rearrange("(i p) d -> p i d", p=P),
                                     xs[:, b * TI:(b + 1) * TI, :]).then_inc(acc_set, 16)
                    if kind == "table":
                        sp.wait_ge(xw_done, b + 1)
                        sp.dma_start(xw_d[b * T:(b + 1) * T, :].rearrange("(i p) d -> p i d", p=P),
                                     xw[:]).then_inc(rows_stored, 16)
                sp.wait_ge(rows_stored, 16 * NB)
                sp.wait_ge(acc_set, 16 * (NSET + NB))

            @block.gpsimd
            def _(pool):
                nc.gpsimd.memset(xw[:], 0.0).then_inc(zero_set, 1)
                nc.gpsimd.memset(half[:], -0.5).then_inc(half_set, 1)
                nc.gpsimd.memset(table[:], 0.0).then_inc(half_set, 1)
                nc.gpsimd.memset(before[:], 0.0).then_inc(half_set, 1)
                for s in range(2):
                    nc.gpsimd.memset(vst[s][:, :, :, 3 * DH:VW], 1.0).then_inc(ones_set, 1)
                pool.wait_ge(half_set, 3)
                norms = [0]

                def root():
                    norms[0] += 1
                    n = norms[0]
                    pool.wait_ge(var_done, n)
                    nc.gpsimd.tensor_scalar(vpe[:], mv[:, :, 1], EPS, None, ALU.add).then_inc(eps_done, 1)
                    pool.wait_ge(eps_done, n)
                    nc.gpsimd.tensor_tensor(rstd[:], vpe[:], half[:], ALU.pow).then_inc(rstd_done, 1)

                for kind, *at in PLAN:
                    b = at.pop(0) if at else None
                    if kind == "norm1":
                        root()
                    if kind == "variance":
                        j, = at
                        i, n = slice(2 * j, 2 * j + 2), 2 * b + j + 1
                        pool.wait_ge(var2_done, n)
                        nc.gpsimd.tensor_scalar(vpe2[:, i], mv2[:, i, 1], EPS, None, ALU.add).then_inc(eps2_done, 1)
                        pool.wait_ge(eps2_done, n)
                        nc.gpsimd.tensor_tensor(rstd2[:, i], vpe2[:, i], half[:, i], ALU.pow).then_inc(rstd2_done, 1)
                    if kind == "sum" and b:
                        rotated(nc.gpsimd, pool, b, *at)
                    if kind == "resid":
                        j, = at
                        n = 4 * b + j
                        pool.wait_ge(part1, n + 1)
                        if n >= 2:
                            pool.wait_ge(part3, n - 1)
                        nc.gpsimd.tensor_tensor(resid[:, j % 2, :], qk[:, j % 2, :], parts[:, 0, j, :],
                                                ALU.subtract).then_inc(residual, 1)
                    if kind == "third" and b:
                        third_part(nc.gpsimd, pool, b, *at)
                    if kind == "second" and on_pool(b * H + at[0]):
                        second_part(nc.gpsimd, pool, b, at[0], p2_pool)

            @block.scalar
            def _(act):
                for kind, *at in PLAN:
                    b = at.pop(0) if at else None
                    if kind == "xnT":
                        ps = wide.wait_full(act, ("xnT", b))
                        if b:
                            wide.wait_full(act, ("v", b - 1, 1))
                        nc.scalar.copy(xT[:, 0, :], ps[:, 0, :])
                        wide.taken(nc.scalar.copy(xT[:, 1, :], ps[:, 1, :]), ("xnT", b))
                    if kind == "first":
                        j, = at
                        if b and j % 2 == 0:
                            act.wait_ge(stored[j // 2], 48 * b)
                        act.wait_ge(summed, 4 * b + j + 1)
                        nc.scalar.copy(parts[:, 0, j, :], qk[:, j % 2, :]).then_inc(part1, 1)
                    if kind == "middle":
                        j, = at
                        act.wait_ge(residual, 4 * b + j + 1)
                        nc.scalar.copy(parts[:, 1, j, :], resid[:, j % 2, :]).then_inc(part2, 1)
                    if kind == "v":
                        j, = at
                        ps = wide.wait_full(act, ("v", b, j))[:, 0]
                        if b >= 2 and j == 0:
                            act.wait_ge(pv_done, H * (b - 1))
                        for i in range(2):
                            ins = nc.scalar.copy(vst[b % 2][:, 2 * j + i, :, 0:DH],
                                                 ps[:, i * D:(i + 1) * D].rearrange("p (h d) -> p h d", d=DH))
                        ins.then_inc(v1_done, 1)
                    if kind == "vrest":
                        j, = at
                        wide.wait_taken(act, ("v", b, j))
                        for i in range(2):
                            ins = nc.scalar.copy(vst[b % 2][:, 2 * j + i, :, DH:2 * DH],
                                                 vres[:, j, i, :].rearrange("p (h d) -> p h d", d=DH))
                        ins.then_inc(v2_done, 1)
                    if kind == "s":
                        h, g = at
                        n = b * H + h
                        ps = narrow.wait_full(act, ("s", b, h, g))
                        if g == 0 and n >= 3:
                            act.wait_ge(pv_done, n - 2)
                        w = sum(T - P * j for j in GROUPS[g])
                        o = POFF[GROUPS[g][0]]
                        narrow.taken(nc.scalar.activation(prob[:, n % 3, o:o + w], ps[:, 0:w], ACT.Exp,
                                                          scale=SCALE), ("s", b, h, g))
                    if kind == "mT":
                        f, = at
                        ps = narrow.wait_full(act, ("mT", b, f))
                        if b:
                            act.wait_ge(m_stored[f], 16 * b)
                        narrow.taken(nc.scalar.copy(mT[f][:], ps[0:H, 0:T // 2].bitcast(BF16)), ("mT", b, f))
                    if kind == "attT":
                        c, = at
                        ps = wide.wait_full(act, ("attT", b, c))[:, 0]
                        wide.taken(nc.scalar.copy(attT[:, c, :], ps), ("attT", b, c))
                    if kind == "x2T":
                        j, = at
                        ps = wide.wait_full(act, ("x2T", b, j))
                        wide.taken(nc.scalar.copy(attT[:, :, j * 2 * P:(j + 1) * 2 * P], ps[:, :, 0:2 * P]),
                                   ("x2T", b, j))
                    if kind == "router":
                        j, = at
                        ps = wide.wait_full(act, ("router", b, j))[:, 0]
                        wide.taken(nc.scalar.copy(lv[:, 2 * j:2 * j + 2, 0:E],
                                                  ps[:, 0:2 * E].rearrange("p (i e) -> p i e", e=E)),
                                   ("router", b, j))
                    if kind == "number":
                        i, = at
                        act.wait_ge(ohe_done, TI * b + i + 1)
                        c, t = slice(i * K, (i + 1) * K), C_TOK + b * TI + i
                        nc.scalar.activation(oht[:, c, :], ohe[:, c, :], ACT.Copy,
                                             scale=consts[:, t:t + 1]).then_inc(oht_done, 1)
                    if kind == "exps":
                        act.wait_ge(lvs_done, b + 1)
                        nc.scalar.activation(ev[:], lv[:], ACT.Exp).then_inc(ev_done, 1)

            @block.tensor
            def _(pe):
                pe.wait_ge(zero_set, 1)
                for n in range(WARM):
                    nc.tensor.matmul(banks[:, 4, :], zeros_b[:, 0:P], zeros_b[:, 0:T], start=True, stop=True)
                pe.wait_ge(cast_done, 1)

                def transposes(key, src, tiles=range(TI), chunks=range(DC)):
                    ps = wide.acquire(pe, key)
                    for r, c in enumerate(chunks):
                        for n, i in enumerate(tiles):
                            ins = nc.tensor.transpose(ps[:, r, n * P:(n + 1) * P], src[:, i, c * P:(c + 1) * P], idf)
                    wide.filled(ins, key)

                def project(key, src, w, chunks=range(DC)):
                    j = key[-1]
                    ps = wide.acquire(pe, key)[:, 0]
                    for i in range(2):
                        for c in chunks:
                            ins = nc.tensor.matmul(ps[:, i * D:(i + 1) * D],
                                                   src[:, c, (2 * j + i) * P:(2 * j + i + 1) * P], w[:, c, :],
                                                   start=(c == chunks[0]), stop=(c == chunks[-1]))
                    wide.filled(ins, key)

                def rotate(b, j):
                    wide.wait_taken(pe, ("xnT", b))
                    if b == 0:
                        pe.wait_ge(w_in, 16 * 5)
                    ps = wide.acquire(pe, ("rope", b, j))
                    for r in range(2):
                        o = j * D + r * P
                        for c in range(DC):
                            ins = nc.tensor.matmul(ps[:, r, :], wqk_sb[:, c, o:o + P], xT[:, c, :],
                                                   start=(c == 0), stop=(c == DC - 1))
                    wide.filled(ins, ("rope", b, j))

                def row_max(b, g, c):
                    s = b % 2
                    if g == 0 and c == 0:
                        pe.wait_ge(loaded[s], 16 * NLOAD * (b // 2 + 1))
                    ps = wide.acquire(pe, ("max", b, g, c))
                    for r, o, h, i in max_blocks(g, c):
                        w = (i + 1) * P
                        nc.tensor.matmul(ps[:, r, o + i * P:o + w], idb, maskq, start=True, stop=False,
                                         skip_group_check=True)
                        ins = nc.tensor.matmul(ps[:, r, o:o + w], stq[s][0:SR, h, i * P:w], stk[s][0:SR, h, 0:w],
                                               start=False, stop=True, skip_group_check=True)
                    wide.filled(ins, ("max", b, g, c))

                def max_rows(b, f):
                    pe.wait_ge(nm_done[f], b + 1)
                    ps = narrow.acquire(pe, ("mT", b, f))[0:H, 0:T // 2].bitcast(BF16)
                    for i in range(TI):
                        ins = nc.tensor.transpose(ps[:, i * P:(i + 1) * P],
                                                  nm[:, i, f, :, :].rearrange("p r h -> p (r h)"), idb)
                    narrow.filled(ins, ("mT", b, f))

                def scores(b, h, g):
                    s = b % 2
                    if b == 0 and h == 0 and g == 0:
                        pe.wait_ge(ones_loaded, 32)
                    if h % (H // 2) == 0 and g == 0:
                        pe.wait_ge(m_loaded[s][h // (H // 2)], 16 * (b // 2 + 1))
                    ps = narrow.acquire(pe, ("s", b, h, g))
                    o = 0
                    for j in GROUPS[g]:
                        w = T - j * P
                        nc.tensor.matmul(ps[:, o:o + P], idb, maskk, start=True, stop=False,
                                         skip_group_check=True)
                        ins = nc.tensor.matmul(ps[:, o:o + w], stk[s][:, h, j * P:(j + 1) * P],
                                               stq[s][:, h, j * P:T], start=False, stop=True,
                                               skip_group_check=True)
                        o += w
                    narrow.filled(ins, ("s", b, h, g))

                def attend_head(b, h):
                    n, s = b * H + h, b % 2
                    if n == 0:
                        pe.wait_ge(ones_set, 2)
                    if h == 0:
                        pe.wait_ge(v3_done, 2 * (b + 1))
                    pe.wait_ge(p2_pool if on_pool(n) else p2_dve, shared_out(n))
                    key = ("out", b, h // 2)
                    ps = outr.acquire(pe, key) if h % 2 == 0 else outr.slot(key)
                    lead, rest = prob_lead(n % 3), prob2[:, n % 3, :]
                    for i in range(TI):
                        o = (h % 2 * TI + i) * VW
                        for j in range(i + 1):
                            c = POFF[j] + (i - j) * P
                            for part in (lead, rest):
                                ins = nc.tensor.matmul(ps[:, o:o + VW], part[:, c:c + P], vst[s][:, j, h, :],
                                                       start=(j == 0 and part is lead),
                                                       stop=(j == i and part is rest), skip_group_check=True)
                        if i == TI - 1:
                            ins.then_inc(pv_done, 1)

                for kind, *at in PLAN:
                    b = at.pop(0) if at else None
                    if kind == "xnT":
                        pe.wait_ge(norm_done, b + 1)
                        transposes(("xnT", b), xn)
                    if kind == "rope":
                        rotate(b, *at)
                    if kind == "v":
                        project(("v", b, *at), xT, wv_sb)
                    if kind == "max":
                        row_max(b, *at)
                    if kind == "mT":
                        max_rows(b, *at)
                    if kind == "s":
                        scores(b, *at)
                    if kind == "pv":
                        attend_head(b, *at)
                    if kind == "attT":
                        c, = at
                        pe.wait_ge(att_done, HP * b + HP // DC * (c + 1))
                        transposes(("attT", b, c), att, chunks=[c])
                    if kind == "proj":
                        c, j = at
                        wide.wait_taken(pe, ("attT", b, c))
                        project(("proj", b, c, j), attT, wp_sb, chunks=[c])
                    if kind == "x2T":
                        j, = at
                        pe.wait_ge(norm2_done, 2 * b + j + 1)
                        transposes(("x2T", b, j), xw, tiles=(2 * j, 2 * j + 1))
                    if kind == "router":
                        j, = at
                        wide.wait_taken(pe, ("x2T", b, j))
                        ps = wide.acquire(pe, ("router", b, j))[:, 0]
                        for i in range(2):
                            for c in range(DC):
                                t = slice((2 * j + i) * P, (2 * j + i + 1) * P)
                                ins = nc.tensor.matmul(ps[:, i * E:(i + 1) * E], attT[:, c, t], wr_sb[:, c, :],
                                                       start=(c == 0), stop=(c == DC - 1))
                        wide.filled(ins, ("router", b, j))
                    if kind == "count":
                        pe.wait_ge(chosen_done, b + 1)
                        ps = wide.acquire(pe, ("count", b))[:, 0]
                        for i in range(TI):
                            nc.tensor.matmul(ps[:, i * E:(i + 1) * E], tri, chosen[:, i, :], start=True, stop=False)
                            for j in range(i):
                                nc.tensor.matmul(ps[:, i * E:(i + 1) * E], onesb, chosen[:, j, :], start=False,
                                                 stop=False)
                            ins = nc.tensor.matmul(ps[:, i * E:(i + 1) * E], onesb, before[:], start=False, stop=True)
                        wide.filled(ins, ("count", b))
                    if kind == "table":
                        ps = wide.acquire(pe, ("table", b))[:, 0]
                        for n in range(TI * K):
                            if n % K == 0:
                                pe.wait_ge(ohc_done, TI * b + n // K + 1)
                                pe.wait_ge(oht_done, TI * b + n // K + 1)
                            ins = nc.tensor.matmul(ps[:, 0:E], ohc[:, n, :], oht[:, n, :], start=(n == 0),
                                                   stop=(n == TI * K - 1))
                        wide.filled(ins, ("table", b))

            @block.vector
            def _(vec):
                v = nc.vector
                step_n = [0]

                def link(ins):
                    step_n[0] += 1
                    ins.then_inc(dve, 1)
                    vec.wait_ge(dve, step_n[0])

                vec.wait_ge(const_in, 16)
                v.tensor_copy(cb[:], consts[:]).then_inc(cast_done, 1)
                norms = [0]

                def normalise(src, dst, done):
                    norms[0] += 1
                    n = norms[0]
                    for i in range(TI):
                        ins = v.bn_stats(stats[:, i, :], src[:, i, :])
                    link(ins)
                    for i in range(TI):
                        ins = v.bn_aggr(mv[:, i, :], stats[:, i, :])
                    ins.then_inc(var_done, 1)
                    vec.wait_ge(rstd_done, n)
                    for i in range(TI):
                        ins = v.tensor_scalar(dst[:, i, 0:D], src[:, i, :], mv[:, i, 0:1], rstd[:, i:i + 1],
                                              ALU.subtract, ALU.mult)
                    ins.then_inc(done, 1)

                def rotate(b, j):
                    n = 2 * b + j
                    if n == 0:
                        vec.wait_ge(w_in, 16 * 5)
                    ps = wide.wait_full(vec, ("rope", b, j))
                    if n:
                        vec.wait_ge(summed, 2 * n)
                    v.tensor_tensor(rc[:, 0], ps[:], rot_sb[:, 0, :].unsqueeze(1).to_broadcast([P, 2, T]), ALU.mult)
                    wide.taken(v.tensor_tensor(rc[:, 1], ps[:], rot_sb[:, 1, :].unsqueeze(1).to_broadcast([P, 2, T]),
                                               ALU.mult), ("rope", b, j))

                def value_residual(b, j):
                    n = 2 * b + j
                    vec.wait_ge(v1_done, n + 1)
                    if n >= 2:
                        vec.wait_ge(v2_done, n - 1)
                        vec.wait_ge(v3_done, n - 1)
                    ps = wide.wait_full(vec, ("v", b, j))[:, 0]
                    for i in range(2):
                        ins = v.tensor_tensor(vres[:, j, i, :].rearrange("p (h d) -> p h d", d=DH),
                                              ps[:, i * D:(i + 1) * D].rearrange("p (h d) -> p h d", d=DH),
                                              vst[b % 2][:, 2 * j + i, :, 0:DH], ALU.subtract)
                    wide.taken(ins, ("v", b, j))

                def value_third(b, j):
                    vec.wait_ge(v2_done, 2 * b + j + 1)
                    for i in range(2):
                        ins = v.tensor_tensor(vst[b % 2][:, 2 * j + i, :, 2 * DH:3 * DH],
                                              vres[:, j, i, :].rearrange("p (h d) -> p h d", d=DH),
                                              vst[b % 2][:, 2 * j + i, :, DH:2 * DH], ALU.subtract)
                    ins.then_inc(v3_done, 1)

                def row_max(b, g, c):
                    ps = wide.wait_full(vec, ("max", b, g, c))
                    if b and g % 2 == 0 and c == 0:
                        vec.wait_ge(nm_done[g // 2], b)
                    if c < 2:
                        h = 4 * g + 2 * c
                        ins = v.tensor_reduce(mx[:, 3, h:h + 2], ps[:], AX_X, ALU.max)
                    elif c < 4:
                        h = 4 * g + 2 * (c - 2)
                        v.tensor_reduce(mx[:, 2, h:h + 2], ps[:, :, 0:3 * P], AX_X, ALU.max)
                        ins = v.tensor_reduce(mx[:, 0, h:h + 2], ps[:, :, 3 * P:4 * P], AX_X, ALU.max)
                    else:
                        ins = v.tensor_reduce(mx[:, 1, 4 * g:4 * g + 4].rearrange("p (r j) -> p r j", r=2),
                                              ps.rearrange("p r (j w) -> p r j w", j=2), AX_X, ALU.max)
                    wide.taken(ins, ("max", b, g, c))

                def negate_max(b, f):
                    for c in (MAX_PIECES - 2, MAX_PIECES - 1):
                        wide.wait_taken(vec, ("max", b, 2 * f + 1, c))
                    if b:
                        narrow.wait_full(vec, ("mT", b - 1, f))
                    m = mx[:, :, f * H // 2:(f + 1) * H // 2]
                    link(v.tensor_scalar(nm[:, :, f, 0, :], m, -1.0, None, ALU.mult))
                    v.scalar_tensor_tensor(out=nm[:, :, f, 1, :], in0=m, scalar=-1.0, in1=nm[:, :, f, 0, :],
                                           op0=ALU.mult, op1=ALU.subtract).then_inc(nm_done[f], 1)

                def finish_pair(b, hp):
                    n = b * HP + hp
                    vec.wait_ge(pv_done, b * H + 2 * hp + 2)
                    ps = outr.slot(("out", b, hp))[:, 0:2 * TI * VW].rearrange("p (g w) -> p g w", w=VW)
                    if n:
                        vec.wait_ge(att_done, n)
                    v.tensor_reduce(red[:], ps[:, :, 0:3 * DH].rearrange("p g (r d) -> p g d r", d=DH), AX_X,
                                    ALU.add)
                    outr.taken(v.reciprocal(rden[:], ps[:, :, 3 * DH]), ("out", b, hp))
                    outr.wait_taken(vec, ("out", b, hp))
                    if hp % (HP // DC) == 0 and b:
                        wide.wait_full(vec, ("attT", b - 1, hp // (HP // DC)))
                    for j in range(2):
                        h = 2 * hp + j
                        ins = v.tensor_tensor(att[:, :, h * DH:(h + 1) * DH], red[:, j * TI:(j + 1) * TI, :],
                                              rden[:, j * TI:(j + 1) * TI].unsqueeze(2).to_broadcast([P, TI, DH]),
                                              ALU.mult)
                    ins.then_inc(att_done, 1)

                def top_eight(b):
                    vec.wait_ge(ranked, 2 * b + 2)
                    for i in range(TI):
                        ins = v.match_replace(lrep[:, i, :], lv[:, i, E:E + K], lv[:, i, 0:E], -3e38)
                    link(ins)
                    v.tensor_tensor(chosen[:], lrep[:], lv[:, :, 0:E], ALU.not_equal).then_inc(chosen_done, 1)
                    link(v.tensor_copy(wsum[:], lv[:, :, E]))
                    v.tensor_tensor(lv[:], lv[:], wsum[:].unsqueeze(2).to_broadcast([P, TI, E + K]),
                                    ALU.subtract).then_inc(lvs_done, 1)

                def weights(b):
                    vec.wait_ge(ev_done, b + 1)
                    link(v.tensor_reduce(wsum[:], ev[:, :, E:E + K], AX_X, ALU.add))
                    link(v.reciprocal(wsum[:], wsum[:]))
                    v.tensor_tensor(xw[:, :, D:XW], ev[:, :, 0:E], wsum[:].unsqueeze(2).to_broadcast([P, TI, E]),
                                    ALU.mult).then_inc(xw_done, 1)

                def choices(b):
                    wide.wait_taken(vec, ("count", b))
                    link(v.tensor_tensor(comp[:], comp[:], chosen[:], ALU.mult))
                    for i in range(TI):
                        ins = v.max(comp8[:, i, :], comp[:, i, :])
                    link(ins)
                    link(v.tensor_copy(compi[:], comp8[:].rearrange("p i k -> p (i k)")))
                    v.tensor_scalar(eki[:, 0, :], compi[:], ESH, None, ALU.logical_shift_right)
                    link(v.tensor_scalar(eki[:, 1, :], compi[:], 2 ** ESH - 1, None, ALU.bitwise_and))
                    v.tensor_copy(ekf[:], eki[:]).then_inc(choices_done, 1)

                def one_hots(b, i):
                    if i == 0:
                        vec.wait_ge(choices_done, b + 1)
                        vec.wait_ge(part3, 4 * min(b + 4, NB))
                    c = slice(i * K, (i + 1) * K)
                    v.tensor_tensor(ohe[:, c, :], consts[:, C_IE:C_IE + E].unsqueeze(1).to_broadcast([P, K, E]),
                                    ekf[:, 0, c].unsqueeze(2).to_broadcast([P, K, E]),
                                    ALU.is_equal).then_inc(ohe_done, 1)
                    v.tensor_tensor(ohc[:, c, :], consts[:, C_IO:C_IO + P].unsqueeze(1).to_broadcast([P, K, P]),
                                    ekf[:, 1, c].unsqueeze(2).to_broadcast([P, K, P]),
                                    ALU.is_equal).then_inc(ohc_done, 1)

                vec.wait_ge(half_set, 3)
                for kind, *at in PLAN:
                    b = at.pop(0) if at else None
                    if kind == "norm1":
                        vec.wait_ge(x_in[b], 16)
                        if b:
                            wide.wait_full(vec, ("xnT", b - 1))
                        normalise(xs[:, b * TI:(b + 1) * TI, :], xn, norm_done)
                    if kind == "rope":
                        rotate(b, *at)
                    if kind == "sum" and b == 0:
                        rotated(v, vec, b, *at)
                    if kind == "third" and b == 0:
                        third_part(v, vec, b, *at)
                    if kind == "v":
                        value_residual(b, *at)
                    if kind == "vrest":
                        value_third(b, *at)
                    if kind == "max":
                        row_max(b, *at)
                    if kind == "negate":
                        negate_max(b, *at)
                    if kind == "second" and not on_pool(b * H + at[0]):
                        second_part(v, vec, b, at[0], p2_dve)
                    if kind == "finish":
                        finish_pair(b, *at)
                    if kind == "proj":
                        c, j = at
                        ps = wide.wait_full(vec, ("proj", b, c, j))[:, 0]
                        if c:
                            wide.wait_taken(vec, ("proj", b, c - 1, j))
                        t = xs[:, b * TI + 2 * j:b * TI + 2 * j + 2, :]
                        wide.taken(v.tensor_tensor(t, t, ps.rearrange("p (i d) -> p i d", d=D), ALU.add),
                                   ("proj", b, c, j))
                    if kind == "variance":
                        j, = at
                        wide.wait_taken(vec, ("proj", b, 1, j))
                        for i in (2 * j, 2 * j + 1):
                            ins = v.bn_stats(stats2[:, i, :], xs[:, b * TI + i, :])
                        link(ins)
                        for i in (2 * j, 2 * j + 1):
                            ins = v.bn_aggr(mv2[:, i, :], stats2[:, i, :])
                        ins.then_inc(var2_done, 1)
                    if kind == "norm2":
                        j, = at
                        if b and j == 0:
                            vec.wait_ge(rows_stored, 16 * b)
                        if b == 0 and j == 0:
                            vec.wait_ge(acc_set, 16 * NSET)
                        vec.wait_ge(rstd2_done, 2 * b + j + 1)
                        for i in (2 * j, 2 * j + 1):
                            ins = v.tensor_scalar(xw[:, i, 0:D], xs[:, b * TI + i, :], mv2[:, i, 0:1],
                                                  rstd2[:, i:i + 1], ALU.subtract, ALU.mult)
                        ins.then_inc(norm2_done, 1)
                    if kind == "rank":
                        j, = at
                        wide.wait_taken(vec, ("router", b, j))
                        for i in (2 * j, 2 * j + 1):
                            ins = v.max(lv[:, i, E:E + K], lv[:, i, 0:E])
                        ins.then_inc(ranked, 1)
                    if kind == "top":
                        top_eight(b)
                    if kind == "count":
                        ps = wide.wait_full(vec, ("count", b))[:, 0]
                        wide.taken(v.tensor_tensor(comp[:], ps[:, 0:TI * E].rearrange("p (i e) -> p i e", e=E),
                                                         consts[:, C_EO:C_EO + E].unsqueeze(1).to_broadcast([P, TI, E]),
                                                         ALU.add), ("count", b))
                        link(v.tensor_reduce(sum4[:], chosen[:].rearrange("p i e -> p e i"), AX_X, ALU.add))
                        link(v.tensor_tensor(before[:], before[:], sum4[:], ALU.add))
                    if kind == "weights":
                        weights(b)
                    if kind == "choice":
                        choices(b)
                    if kind == "onehot":
                        one_hots(b, *at)
                    if kind == "table":
                        ps = wide.wait_full(vec, ("table", b))[:, 0]
                        wide.taken(v.tensor_tensor(table[:], table[:], ps[:, 0:E], ALU.add), ("table", b))
                        wide.wait_taken(vec, ("table", b))
                v.tensor_scalar(rows_of[:, :, 0], table[:], -1.0, 0.0, ALU.add, ALU.max)
                link(v.tensor_scalar(comp[:, 0, :], table[:], 0.0, consts[:, C_DUM:C_DUM + 1], ALU.is_equal, ALU.mult))
                v.scalar_tensor_tensor(out=rows_of[:, :, 1], in0=table[:], scalar=-1.0, in1=comp[:, 0, :],
                                       op0=ALU.add, op1=ALU.add).then_inc(rows_done, 1)


def experts(nc, xw_d, acc_d, banks, idf, rows_of, gup_v, dnp_v):
    ctx = ExitStack()
    with ctx:
        def sb(name, shape, dt):
            return ctx.enter_context(nc.sbuf_tensor(name, shape, dt))

        def sem(name):
            return ctx.enter_context(nc.semaphore(name))

        gup_sb = sb("gup_sb", [P, U, 2, 2 * I], F32)
        dnp_sb = sb("dnp_sb", [I, U, D], F32)
        gath = sb("gath", [P, U, XW], F32)
        xTe = sb("xTe", [P, 2, DC, P], F32)
        gate = sb("gate", [I, 2, P], F32)
        hid = sb("hid", [I, 2, P], F32)
        wcol = sb("wcol", [P, U], F32)
        warm = sb("warm", [P, 1], F32)
        ye = sb("ye", [P, U, D], F32)
        psX = [banks[:, n, 0:DC * P].rearrange("p (c n) -> p c n", c=DC) for n in (0, 1)]
        psG = [banks[0:I, n, 0:2 * P].rearrange("p (c n) -> p c n", c=2) for n in (2, 3)]
        psY = [banks[:, n, 0:D] for n in (4, 5)]

        gup_in = [sem(f"gup_in{s}") for s in range(U)]
        dnp_in = [sem(f"dnp_in{s}") for s in range(U)]
        gath_in = [sem(f"gath_in{s}") for s in range(U)]
        x_turned, x_copied = sem("x_turned"), sem("x_copied")
        gu_done, gate_done, hid_done = sem("gu_done"), sem("gate_done"), sem("hid_done")
        down_done, cols_done, y_done = sem("down_done"), sem("cols_done"), sem("y_done")
        added = [sem(f"added{a}") for a in range(NACC)]
        out_set = sem("out_set")

        def wait(eng, s, value):
            if not isinstance(value, int) or value > 0:
                eng.wait_ge(s, value)

        def rounds(eng, body):
            body(0, False)
            with eng.Fori(1, NR - 1) as k:
                body(k, False)
            body(NR - 1, True)

        with nc.Block() as block:
            @block.sync
            def _(sp):
                for s in range(U):
                    sp.dma_start(gup_sb[:, s], gup_v[:, s]).then_inc(gup_in[s], 16)
                    sp.dma_start(dnp_sb[:, s], dnp_v[:, s]).then_inc(dnp_in[s], 16)

                def body(k, last):
                    if last:
                        return
                    for s in range(U):
                        sp.wait_ge(down_done, k * U + s + 1)
                        sp.dma_start(gup_sb[:, s:s + 1], gup_v[:, bass.ds(k * U + s + U, 1)]).then_inc(gup_in[s], 16)
                        sp.dma_start(dnp_sb[:, s:s + 1], dnp_v[:, bass.ds(k * U + s + U, 1)]).then_inc(dnp_in[s], 16)

                rounds(sp, body)

            @block.gpsimd
            def _(pool):
                last_row = nc.gpsimd.to_reg(NTOK - 1)
                last_acc = nc.gpsimd.to_reg(ROWS - 1)

                def gather(n):
                    nc.gpsimd.indirect_dma_start(
                        out=gath[:, n % U, :], out_offset=None, in_=xw_d,
                        in_offset=bass.IndirectOffsetOnAxis(ap=rows_of[:, n, 0:1], axis=0),
                        bounds_check=last_row, oob_is_err=False).then_inc(gath_in[n % U], 16)

                for n in range(U):
                    gather(n)
                for n in range(E):
                    a = n % NACC
                    pool.wait_ge(y_done, n + 1)
                    if n >= NACC:
                        pool.wait_ge(added[a], 16 * (n // NACC))
                    nc.gpsimd.indirect_dma_start(
                        out=acc_d[a], out_offset=bass.IndirectOffsetOnAxis(ap=rows_of[:, n, 1:2], axis=0),
                        in_=ye[:, n % U, :], in_offset=None,
                        bounds_check=last_acc, oob_is_err=True, compute_op=ALU.add).then_inc(added[a], 16)
                    if n + U < E:
                        gather(n + U)
                for a in range(NACC):
                    pool.wait_ge(added[a], 16 * (E // NACC))
                for a in range(1, NACC):
                    if a > 1:
                        pool.wait_ge(out_set, 16 * SUMS * (a - 1))
                    for c in range(SUMS):
                        to, what = [t[0:NTOK, :].rearrange("(p r) d -> p (r d)", p=P)
                                    [:, c * NT * D // SUMS:(c + 1) * NT * D // SUMS] for t in (acc_d[0], acc_d[a])]
                        nc.gpsimd.dma_start(to, what, accum_op=ALU.add).then_inc(out_set, 16)
                pool.wait_ge(out_set, 16 * SUMS * (NACC - 1))

            @block.scalar
            def _(act):
                def copy_x(n, s):
                    act.wait_ge(x_turned, n + 1)
                    wait(act, gu_done, n - 1)
                    nc.scalar.copy(xTe[:, s % 2], psX[s % 2]).then_inc(x_copied, 1)

                def silu(n, s):
                    act.wait_ge(gu_done, n + 1)
                    wait(act, hid_done, n - 1)
                    nc.scalar.activation(gate[:, s % 2], psG[s % 2][:, 0], ACT.Silu).then_inc(gate_done, 1)

                nc.scalar.activation(warm[:], idf[:, 0:1], ACT.Silu)
                copy_x(0, 0)
                copy_x(1, 1)
                silu(0, 0)

                def body(k, last):
                    for s in range(U):
                        n = k * U + s
                        if not last or s + 2 < U:
                            copy_x(n + 2, s)
                        if not last or s + 1 < U:
                            silu(n + 1, s + 1)

                rounds(act, body)

            @block.tensor
            def _(pe):
                def turn(n, s, k):
                    pe.wait_ge(gath_in[s % U], 16 * (k + s // U + 1))
                    wait(pe, x_copied, n - 1)
                    rows = gath[:, s % U, 0:D].rearrange("p (n c) -> p c n", c=DC)
                    for c in range(DC):
                        ins = nc.tensor.transpose(psX[s % 2][:, c, :], rows[:, c, :], idf)
                    ins.then_inc(x_turned, 1)

                def gate_up(n, s, k):
                    pe.wait_ge(x_copied, n + 1)
                    pe.wait_ge(gup_in[s % U], 16 * (k + s // U + 1))
                    wait(pe, hid_done, n - 1)
                    for r in range(2):
                        for c in range(DC):
                            ins = nc.tensor.matmul(psG[s % 2][:, r, :], gup_sb[:, s % U, c, r * I:(r + 1) * I],
                                                   xTe[:, s % 2, c, :], start=(c == 0), stop=(c == DC - 1))
                    ins.then_inc(gu_done, 1)

                def down(n, s, k):
                    pe.wait_ge(hid_done, n + 1)
                    pe.wait_ge(dnp_in[s], 16 * (k + 1))
                    wait(pe, y_done, n - 1)
                    nc.tensor.matmul(psY[s % 2], hid[:, s % 2, :], dnp_sb[:, s, :], start=True,
                                     stop=True).then_inc(down_done, 1)

                turn(0, 0, 0)
                turn(1, 1, 0)
                gate_up(0, 0, 0)

                def body(k, last):
                    for s in range(U):
                        n = k * U + s
                        if not last or s + 2 < U:
                            turn(n + 2, s + 2, k)
                        if not last or s + 1 < U:
                            gate_up(n + 1, s + 1, k)
                        down(n, s, k)

                rounds(pe, body)

            @block.vector
            def _(vec):
                v = nc.vector

                def hidden(n, s):
                    vec.wait_ge(gate_done, n + 1)
                    wait(vec, down_done, n - 1)
                    v.tensor_tensor(hid[:, s % 2], gate[:, s % 2], psG[s % 2][:, 1], ALU.mult).then_inc(hid_done, 1)

                def weigh(n, s, k):
                    if not isinstance(k, int) or k > 0:
                        vec.wait_ge(added[s % NACC], 16 * ((k - 1) * (U // NACC) + s // NACC + 1))
                    vec.wait_ge(gath_in[s], 16 * (k + 1))
                    v.tensor_copy(wcol[:, s:s + 1], gath[:, s, bass.ds(n + D, 1)]).then_inc(cols_done, 1)
                    vec.wait_ge(down_done, n + 1)
                    vec.wait_ge(cols_done, n + 1)
                    v.tensor_scalar(ye[:, s, :], psY[s % 2], wcol[:, s:s + 1], None, ALU.mult).then_inc(y_done, 1)

                hidden(0, 0)

                def body(k, last):
                    for s in range(U):
                        n = k * U + s
                        if not last or s + 1 < U:
                            hidden(n + 1, s + 1)
                        weigh(n, s, k)

                rounds(vec, body)


def kernel(**inputs):
    import concourse.bacc as _bacc
    from concourse.bass_utils import run_bass_kernel_spmd as _run

    x = np.asarray(inputs["L0_attn_x"])
    w = np.asarray(inputs["L0_attn_w_qkv"])
    by_place = np.arange(2 * D).reshape(2, H, DH).transpose(0, 2, 1).reshape(-1)
    wt = w.T
    cst, rot = constants()
    arrays = {
        "in_x": np.ascontiguousarray(x.reshape(NTOK, D)),
        "in_wqk": np.ascontiguousarray(wt[:, by_place]),
        "in_wv": np.ascontiguousarray(wt[:, 2 * D:]),
        "in_wp": np.ascontiguousarray(np.asarray(inputs["L0_attn_w_proj"]).T),
        "in_wr": np.ascontiguousarray(np.asarray(inputs["L0_ffn_router_weight"]).T),
        "in_gup": np.ascontiguousarray(inputs["L0_ffn_gate_up_proj"]),
        "in_dnp": np.ascontiguousarray(inputs["L0_ffn_down_proj"]),
        "in_cst": cst,
        "in_rot": rot,
    }
    nc = _bacc.Bacc("TRN2", target_bir_lowering=False, num_devices=1)
    args = [nc.dram_tensor(n, a.shape, mybir.dt.from_np(a.dtype), kind="ExternalInput").ap()
            for n, a in arrays.items()]
    args.append(nc.dram_tensor("out_y", (ROWS, D), F32, kind="ExternalOutput").ap())
    build(nc, *args)
    r = _run(nc, [arrays], core_ids=[0])
    return r.results[0]["out_y"][:NTOK].reshape(x.shape)
```
